# Optimizing a Trainium2 kernel written in Bass

```python
import numpy as np
import jax
import jax.numpy as jnp

def _softmax(x, axis=-1):
    return jax.nn.softmax(x, axis=axis)

def _gelu(x):
    return jax.nn.gelu(x, approximate=True)

def _silu(x):
    return jax.nn.silu(x)

def _sigmoid(x):
    return jax.nn.sigmoid(x)

def _layernorm(x, axis=-1, eps=1e-05):
    m = jnp.mean(x, axis=axis, keepdims=True)
    v = jnp.var(x, axis=axis, keepdims=True)
    return (x - m) / jnp.sqrt(v + eps)

def _scatter_add(tgt, idx, src, axis=0):
    return tgt.at[idx].add(src)

def _segment_sum(src, seg, n):
    return jax.ops.segment_sum(src, seg, n)
kernel_name = 'mk_flamingo_gated_d1_seqx_r8_de6554'

def setup_inputs(seed: int=0):
    np.random.seed(seed)
    _w = jnp.asarray

    def _rec_inputs():
        import jax
        import jax.numpy as jnp
        _rk = jax.random.key(seed)
        x = 0.0003765 + 1 * jax.random.normal(jax.random.fold_in(_rk, 1), (16, 128, 256), jnp.float32)
        _lenS = 128 - jax.random.randint(jax.random.fold_in(_rk, 7), (16,), 0, max(1, 128 // 4) + 1, jnp.int32)
        _lenS2 = 128 - jax.random.randint(jax.random.fold_in(_rk, 8), (16,), 0, max(1, 128 // 4) + 1, jnp.int32)
        _ctx_2048P = jax.random.normal(jax.random.fold_in(_rk, 11), (16, 16, 256), jnp.float32)
        _ctx_2048c = jax.random.dirichlet(jax.random.fold_in(_rk, 511), 0.3 * jnp.ones((16,), jnp.float32), (16, 128))
        _ctx_2048t = jnp.einsum('bsk,bkd->bsd', _ctx_2048c, _ctx_2048P)
        _ctx_2048t = _ctx_2048t * jax.lax.rsqrt(jnp.mean(jnp.square(_ctx_2048t)) + 1e-12) * 0.953939
        ctx_2048 = -0.000292821 + 1.00034 * (_ctx_2048t + 0.3 * jax.random.normal(jax.random.fold_in(_rk, 611), (16, 128, 256), jnp.float32))
        _g = jax.random.normal(jax.random.fold_in(_rk, 9001), (2, 1), jnp.float32)
        _g = jnp.sign(_g) * jnp.maximum(jnp.abs(_g), 1.0) + (_g == 0) * 1.0
        g_xattn = _g[0]
        g_ffn = _g[1]
        return (x, ctx_2048, g_xattn, g_ffn)
    x, ctx_2048, g_xattn, g_ffn = _rec_inputs()

    def _L0_xattn_setup():
        import jax, jax.numpy as jnp
        import numpy as np
        key = jax.random.key(seed)
        k1, k2, k3, k4, k5 = jax.random.split(key, 5)
        B, D_MODEL, L = (2, 128, 256)
        HEAD_DIM = 8
        H = D_MODEL // HEAD_DIM
        return {'k': jax.random.normal(k1, (B, D_MODEL, L), dtype=jnp.float32), 'v': jax.random.normal(k2, (B, D_MODEL, L), dtype=jnp.float32), 'q': jax.random.normal(k3, (B, D_MODEL, L), dtype=jnp.float32), 'ssm_kernel': jax.random.normal(k4, (H, L), dtype=jnp.float32), 'D': jax.random.normal(k5, (H,), dtype=jnp.float32), 'head_dim': HEAD_DIM}
    _L0_xattn_all = _L0_xattn_setup()
    _L0_xattn_in = {k: v for k, v in _L0_xattn_all.items() if k in ('ssm_kernel', 'D')}
    del _L0_xattn_all

    def _L0_ffn_setup():
        import jax, jax.numpy as jnp
        import numpy as np
        BS, SLEN, DIM, HID, E, K = (2, 128, 256, 128, 8, 2)
        INIT_STD = 0.02
        key = jax.random.key(seed)
        ks = jax.random.split(key, 8)
        s = INIT_STD
        return {'x': jax.random.normal(ks[0], (BS, SLEN, DIM), jnp.float32), 'gate_w': jax.random.normal(ks[1], (E, DIM), jnp.float32) * s, 'w1': jax.random.normal(ks[2], (E, HID, DIM), jnp.float32) * s, 'w2': jax.random.normal(ks[3], (E, DIM, HID), jnp.float32) * s, 'w3': jax.random.normal(ks[4], (E, HID, DIM), jnp.float32) * s, 'sw1': jax.random.normal(ks[5], (HID, DIM), jnp.float32) * s, 'sw2': jax.random.normal(ks[6], (DIM, HID), jnp.float32) * s, 'sw3': jax.random.normal(ks[7], (HID, DIM), jnp.float32) * s}
    _L0_ffn_all = _L0_ffn_setup()
    _L0_ffn_in = {k: v for k, v in _L0_ffn_all.items() if k in ('gate_w', 'w1', 'w2', 'w3', 'sw1', 'sw2', 'sw3')}
    del _L0_ffn_all
    return {'x': x, 'ctx_2048': ctx_2048, 'g_xattn': g_xattn, 'g_ffn': g_ffn, 'L0_xattn_ssm_kernel': _L0_xattn_in['ssm_kernel'], 'L0_xattn_D': _L0_xattn_in['D'], 'L0_ffn_gate_w': _L0_ffn_in['gate_w'], 'L0_ffn_w1': _L0_ffn_in['w1'], 'L0_ffn_w2': _L0_ffn_in['w2'], 'L0_ffn_w3': _L0_ffn_in['w3'], 'L0_ffn_sw1': _L0_ffn_in['sw1'], 'L0_ffn_sw2': _L0_ffn_in['sw2'], 'L0_ffn_sw3': _L0_ffn_in['sw3']}

def reference(x, ctx_2048, g_xattn, g_ffn, L0_xattn_ssm_kernel, L0_xattn_D, L0_ffn_gate_w, L0_ffn_w1, L0_ffn_w2, L0_ffn_w3, L0_ffn_sw1, L0_ffn_sw2, L0_ffn_sw3):
    import jax
    import jax.numpy as jnp

    def _L0_xattn_ref(k, v, q, ssm_kernel, D, head_dim):
        import jax, jax.numpy as jnp
        import numpy as np
        B, HD, L = k.shape
        H = HD // head_dim
        fft_size = 2 * L
        k_ = k.reshape(B, H, head_dim, L)
        v_ = v.reshape(B, H, head_dim, L)
        q_ = q.reshape(B, H, head_dim, L)
        kv = jnp.einsum('bhil,bhjl->bijhl', k_, v_)
        kv_f = jnp.fft.rfft(kv, n=fft_size)
        kernel_f = jnp.fft.rfft(ssm_kernel, n=fft_size)
        y = jnp.fft.irfft(kv_f * kernel_f, n=fft_size)[..., :L]
        out = y + kv * D[None, None, None, :, None]
        out = jnp.einsum('bijhl,bhil->bjhl', out, q_)
        out = jnp.transpose(out, (0, 2, 1, 3)).reshape(B, H * head_dim, L)
        return out.astype(k.dtype)

    def _L0_ffn_ref(x, gate_w, w1, w2, w3, sw1, sw2, sw3):
        import jax, jax.numpy as jnp
        import numpy as np
        BS, SLEN, DIM, HID, E, K = (2, 128, 256, 128, 8, 2)
        INIT_STD = 0.02
        bs, slen, dim = x.shape
        xt = x.reshape(-1, dim)
        scores = jax.nn.sigmoid((xt @ gate_w.T).astype(jnp.float32))
        top_scores, sel = jax.lax.top_k(scores, K)
        flat_sel = sel.reshape(-1)
        order = jnp.argsort(flat_sel, stable=True)
        token_idx = order // K
        expert_sorted = flat_sel[order]
        slot_scores = top_scores.reshape(-1)[order]
        routed_x = xt[token_idx] * slot_scores[:, None].astype(xt.dtype)
        out_r = jnp.zeros_like(routed_x)
        for e in range(E):
            m = (expert_sorted == e)[:, None].astype(routed_x.dtype)
            h = jax.nn.silu(routed_x @ w1[e].T) * (routed_x @ w3[e].T)
            out_r = out_r + h @ w2[e].T * m
        shared = jax.nn.silu(xt @ sw1.T) * (xt @ sw3.T) @ sw2.T
        out = shared.at[token_idx].add(out_r)
        return out.reshape(bs, slen, dim)
    x = x + jnp.tanh(g_xattn[0]) * _L0_xattn_ref(ctx_2048, ctx_2048, _layernorm(x, axis=-1), L0_xattn_ssm_kernel, L0_xattn_D, 8)
    x = x + jnp.tanh(g_ffn[0]) * _L0_ffn_ref(_layernorm(x, axis=-1), L0_ffn_gate_w, L0_ffn_w1, L0_ffn_w2, L0_ffn_w3, L0_ffn_sw1, L0_ffn_sw2, L0_ffn_sw3)
    return x

_drawn_inputs = setup_inputs


def setup_inputs(seed=0):
    import zlib

    import numpy as np

    out = dict(_drawn_inputs(seed))
    spreads = {}
    factors = {'L0_ffn_gate_w': 8.0,
     'L0_ffn_w1': 8.0,
     'L0_ffn_w2': 8.0,
     'L0_ffn_w3': 8.0,
     'L0_ffn_sw1': 8.0,
     'L0_ffn_sw2': 8.0,
     'L0_ffn_sw3': 8.0}
    for name, (base, spread) in spreads.items():
        noise = np.random.default_rng([zlib.crc32(name.encode()), seed]).standard_normal(out[name].shape)
        drawn = base * np.exp(spread * noise) if base else spread * noise
        out[name] = jnp.asarray(drawn.astype(out[name].dtype))
    for name, factor in factors.items():
        out[name] = (out[name] * factor).astype(out[name].dtype)
    return out
```

```python
from contextlib import ExitStack

import concourse.bass as bass
from concourse import mybir

ALU = mybir.AluOpType
ACT = mybir.ActivationFunctionType
F32 = mybir.dt.float32
BF16 = mybir.dt.bfloat16
I32 = mybir.dt.int32
U32 = mybir.dt.uint32
AX_X = mybir.AxisListType.X

P = 128
H = 16
B = 16
HD = 8
L = 256
LB = L // P
E = 8
TOPK = 2
HID = 128
EPS = 1e-5

D_FULL = HD // 2
PAIRS = D_FULL * B * HD
PAIRS4 = B * HD // 2
ZW = PAIRS + PAIRS4
KW = HD + D_FULL
YW = HD + D_FULL - 1
YPAD = D_FULL - 1
QW = 16
ROWS = B * HD

CHUNK = 4
NCHUNK = H // CHUNK
SLOTS = H * ROWS * TOPK
TILES = SLOTS // P + E - 1
KPAD = 384
ROUND = 4


class Turn:

    def __init__(self, i, k):
        self.i, self.k = i + k // 2, k % 2
        self.n = self.i * 2 + self.k
        self.slot = self.k

    def __add__(self, d):
        return Turn(self.i, self.k + d)

    def __sub__(self, d):
        return Turn(self.i, self.k - d)


def await_count(eng, sem, n):
    if not isinstance(n, int) or n > 0:
        eng.wait_ge(sem, n)


def run_steps(eng, step, first, last, steady_first, steady_last):
    assert steady_first % 2 == 0 and (steady_last - steady_first) % 2 == 1
    for n in range(first, steady_first):
        step(Turn(n // 2, n % 2))
    with eng.Fori(steady_first // 2, (steady_last + 1) // 2) as i:
        for k in range(2):
            step(Turn(i, k))
    for n in range(steady_last + 1, last + 1):
        step(Turn(n // 2, n % 2))


def view(tensor, offset, dims):
    whole = tensor[:]
    return bass.AP(whole.tensor, offset + whole.offset, [list(whole.ap[0])] + [list(d) for d in dims])


def flamingo_block(nc, x, ctx, g_xattn, g_ffn, taps, skip, gate_w, w13, w2, sw13, sw2, out):
    filt_dram = nc.dram_tensor("filt_dram", [H, KPAD], F32, kind="Internal").ap()
    routed_in = nc.dram_tensor("routed_in", [TILES * P, L], F32, kind="Internal").ap()
    routed_out = nc.dram_tensor("routed_out", [TILES * P, L], F32, kind="Internal").ap()

    with ExitStack() as stack:
        def sb(name, shape, dt=F32):
            return stack.enter_context(nc.sbuf_tensor(name, shape, dt))

        def sem(name):
            return stack.enter_context(nc.semaphore(name))

        ident = sb("ident", [P, P])
        before = sb("before", [P, P], BF16)
        ones = sb("ones", [P, P], BF16)
        ones_row = sb("ones_row", [P, E])
        down = sb("down", [P, E])
        fills = sb("fills", [P, H])
        tile_id = sb("tile_id", [P, TILES])
        eps = sb("eps", [P, 1])
        zeros = sb("zeros", [P, L])
        gates = sb("gates", [P, 2])
        tanh_g = sb("tanh_g", [P, 2])
        filt = sb("filt", [H, KPAD])
        skip_sb = sb("skip_sb", [H, 1])
        gate_sb = sb("gate_sb", [P, LB, E])
        w13_sb = sb("w13_sb", [P, LB, E * 2 * HID])
        w2_sb = sb("w2_sb", [P, E * L])
        sw13_sb = sb("sw13_sb", [P, LB, 2 * HID])
        sw2_sb = sb("sw2_sb", [P, L])
        x_all = sb("x_all", [P, H * L])
        base_all = sb("base_all", [P, H * L])
        xnT_all = sb("xnT_all", [P, LB, H * P])
        st1 = sb("st1", [P, H, 6])
        mean1 = sb("mean1", [P, H])
        var1 = sb("var1", [P, H])
        half1 = sb("half1", [P, H])
        std1 = sb("std1", [P, H])
        rstd1 = sb("rstd1", [P, H])
        keys = sb("keys", [P, 2, LB, B * KW])
        toep = sb("toep", [P, 2, L])
        z = sb("z", [P, 2, LB, ZW])
        xq = sb("xq", [P, 2, L])
        queries = sb("queries", [P, 2, LB, B * QW])
        y = sb("y", [P, 2, LB, (D_FULL + 1) * B * YW])
        prods = sb("prods", [P, LB, ROWS * HD])
        att = sb("att", [P, 2, LB, ROWS])
        st2 = sb("st2", [P, 2, 6])
        mv2 = sb("mv2", [P, 2, 2])
        std2 = sb("std2", [P, 2])
        mean_all = sb("mean_all", [P, H])
        rstd_all = sb("rstd_all", [P, H])
        xn = sb("xn", [P, 2, L])
        xnT = sb("xnT", [P, 2, LB, P])
        logits = sb("logits", [P, H * E])
        probs = sb("probs", [P, H, E])
        score = sb("score", [P, H, TOPK])
        is_max = sb("is_max", [P, H, E])
        rank = sb("rank", [P, H, E])
        top_rank = sb("top_rank", [P, H, TOPK])
        chosen = sb("chosen", [P, TOPK, H, E])
        rest = sb("rest", [P, H, E])
        mask = sb("mask", [P, H * E], BF16)
        count = sb("count", [P, E])
        over = sb("over", [P, E, H])
        tiles = sb("tiles", [P, E])
        tiles_to = sb("tiles_to", [P, E])
        tiles_before = sb("tiles_before", [P, E])
        place = sb("place", [P, H, E])
        picked = sb("picked", [P, TOPK, H, E])
        slot_f = sb("slot_f", [P, H, TOPK])
        slot_of = sb("slot_of", [P, H, TOPK], I32)
        ended = sb("ended", [1, TILES, E])
        tile_expert_f = sb("tile_expert_f", [1, TILES])
        tile_expert = sb("tile_expert", [1, TILES], I32)
        xn_again = sb("xn_again", [P, 2, L])
        rows = sb("rows", [P, ROUND, TOPK, L])
        shared_act = sb("shared_act", [P, 2, CHUNK * P])
        shared_h = sb("shared_h", [P, 2, CHUNK * P])
        r_in = sb("r_in", [P, 2, L])
        r_inT = sb("r_inT", [P, 2, LB, P])
        r_act = sb("r_act", [P, 2, HID])
        r_h = sb("r_h", [P, 2, HID])
        r_hT = sb("r_hT", [P, 2, P])
        r_out = sb("r_out", [P, 2, L])
        both = sb("both", [P, 2, L])
        result = sb("result", [P, ROUND, L])

        banks = [stack.enter_context(nc.psum_tensor(f"bank{n}", [P, 512], F32)) for n in range(8)]
        y_ps = [banks[0], banks[1]]
        y4_ps = [banks[2][:, 0:PAIRS4], banks[3][:, 0:PAIRS4]]
        q_ps = banks[4][:, 0:L]
        att_ps = banks[5][:, 0:L]
        xnT_ps = banks[6][:, 0:L]
        gate_ps = banks[7][:, 0:E]
        place_ps = banks[4][:, 0:H * E]
        total_ps = banks[4][:, 256:256 + H * E]
        up_ps = [[banks[0], banks[1]], [banks[2], banks[3]]]
        sh_ps = [banks[4 + t][:, 0:L] for t in range(CHUNK)]
        rT_ps = [banks[0 + s][:, 0:256] for s in range(2)]
        ru_ps = [banks[2 + s][:, 0:256] for s in range(2)]
        rh_ps = [banks[4 + s][:, 0:P] for s in range(2)]
        ro_ps = [banks[6 + s][:, 0:256] for s in range(2)]

        x_loaded = [sem(f"x_loaded{c}") for c in range(4)]
        small_loaded = sem("small_loaded")
        gates_loaded = sem("gates_loaded")
        gatew_loaded = sem("gatew_loaded")
        shared_loaded = sem("shared_loaded")
        experts_loaded = sem("experts_loaded")
        filt_ready = sem("filt_ready")
        filt_zeroed = sem("filt_zeroed")
        filt_stored = sem("filt_stored")
        keys_loaded = [sem(f"keys_loaded{s}") for s in range(2)]
        toep_loaded = [sem(f"toep_loaded{s}") for s in range(2)]
        zeros_ready = sem("zeros_ready")
        rows_zeroed = sem("rows_zeroed")
        pool_const = sem("pool_const")
        consts_ready = sem("consts_ready")
        eps_ready = sem("eps_ready")
        tanh_ready = sem("tanh_ready")
        norm1 = sem("norm1")
        var1_ready = sem("var1_ready")
        std1_ready = sem("std1_ready")
        z_ready = sem("z_ready")
        y_done_b = sem("y_done_b")
        y_ready_b = sem("y_ready_b")
        near_done_b = sem("near_done_b")
        far_done_b = sem("far_done_b")
        att_ready_b = sem("att_ready_b")
        xq_ready = sem("xq_ready")
        q_done = sem("q_done")
        q_ready = sem("q_ready")
        att_done = sem("att_done")
        x1_ready = sem("x1_ready")
        mv_ready = sem("mv_ready")
        std_ready = sem("std_ready")
        rstd_ready = sem("rstd_ready")
        xn_ready = sem("xn_ready")
        xnT_done = sem("xnT_done")
        xnT_ready = sem("xnT_ready")
        gate_done = sem("gate_done")
        logits_ready = sem("logits_ready")
        probs_ready = sem("probs_ready")
        route = sem("route")
        mask_ready = sem("mask_ready")
        place_done = sem("place_done")
        slots_ready = sem("slots_ready")
        table_ready = sem("table_ready")
        up_done = sem("up_done")
        sact_ready = sem("sact_ready")
        sh_ready = sem("sh_ready")
        sout_done = sem("sout_done")
        base_ready = sem("base_ready")
        again_ready = sem("again_ready")
        rows_ready = sem("rows_ready")
        scattered = [sem(f"scattered{s}") for s in range(ROUND)]
        r_loaded = [sem(f"r_loaded{s}") for s in range(2)]
        rT_done = sem("rT_done")
        rT_ready = sem("rT_ready")
        ru_done = sem("ru_done")
        ract_ready = sem("ract_ready")
        rh_ready = sem("rh_ready")
        rhT_done = sem("rhT_done")
        rhT_ready = sem("rhT_ready")
        ro_done = sem("ro_done")
        ro_ready = sem("ro_ready")
        r_stored = [sem(f"r_stored{s}") for s in range(2)]
        gathered = [sem(f"gathered{s}") for s in range(ROUND)]
        both_ready = sem("both_ready")
        result_ready = sem("result_ready")
        out_stored = [sem(f"out_stored{s}") for s in range(ROUND)]

        block = stack.enter_context(nc.Block())

        def head_rows(t, n):
            return t[:, bass.ds(n * L, L)]

        @block.sync
        def _(sp):
            sp.dma_start(filt[:, P - 1:P - 1 + L], taps).then_inc(small_loaded, 16)
            sp.dma_start(skip_sb[:, :], skip).then_inc(small_loaded, 16)
            for c in range(4):
                w = H * L // 4
                sp.dma_start(x_all[:, c * w:(c + 1) * w], x[:, c * w:(c + 1) * w]).then_inc(x_loaded[c], 16)
                if c == 0:
                    for s in range(2):
                        sp.dma_start(keys[:, s], ctx[s]).then_inc(keys_loaded[s], 16)
            sp.wait_ge(filt_ready, 1)
            sp.dma_start(filt_dram, filt[:, :]).then_inc(filt_stored, 16)
            sp.wait_ge(filt_stored, 16)

            def load_toep(h):
                src = bass.AP(filt_dram.tensor, h.n * KPAD, [[1, P], [1, L]])
                sp.dma_start(toep[:, h.slot], src).then_inc(toep_loaded[h.slot], 16)

            for s in range(2):
                load_toep(Turn(0, s))

            def step(h):
                await_count(sp, z_ready, (h - 2).n + 1)
                sp.dma_start(keys[:, h.slot], ctx[bass.ds(h.n, 1)].rearrange("a p b c -> p (a b) c"))\
                    .then_inc(keys_loaded[h.slot], 16)
                await_count(sp, y_done_b, ((h - 2).n + 1) * LB)
                load_toep(h)

            with sp.Fori(1, H // 2) as i:
                for k in range(2):
                    step(Turn(i, k))

            for s in range(ROUND):
                sp.wait_ge(scattered[s], 16 * TOPK * (H // ROUND))
            sp.wait_ge(rows_zeroed, 16)

            def load_tile(t):
                src = routed_in[bass.ds(t.n * P, P), :]
                sp.dma_start(r_in[:, t.slot], src).then_inc(r_loaded[t.slot], 16)

            def routed(t, load=True):
                if load:
                    await_count(sp, rT_done, (t - 1).n)
                    load_tile(t)
                if not isinstance(t.n, int) or t.n >= 4:
                    u = t - 4
                    sp.wait_ge(ro_ready, u.n + 1)
                    sp.dma_start(routed_out[bass.ds(u.n * P, P), :], r_out[:, u.slot])\
                        .then_inc(r_stored[u.slot], 16)

            for n in range(4):
                routed(Turn(n // 2, n % 2))
            with sp.Fori(2, (TILES - 1) // 2) as i:
                for k in range(2):
                    routed(Turn(i, k))
            for n in range(TILES - 1, TILES + 4):
                routed(Turn(n // 2, n % 2), load=n < TILES)

            for n in range(H):
                sp.wait_ge(result_ready, n + 1)
                sp.dma_start(out[:, n * L:(n + 1) * L], result[:, n % ROUND]).then_inc(out_stored[n % ROUND], 16)
            for s in range(ROUND):
                sp.wait_ge(out_stored[s], 16 * (H // ROUND))

        @block.gpsimd
        def _(pool):
            def make_z(h):
                pool.wait_ge(keys_loaded[h.slot], h.i * 16 + 16)
                await_count(pool, y_done_b, ((h - 2).n + 1) * LB)
                for b in range(LB):
                    at = (h.slot * LB + b) * B * KW
                    nc.gpsimd.tensor_tensor(
                        z[:, h.slot, b, 0:PAIRS].rearrange("p (d b i) -> p d b i", d=D_FULL, b=B),
                        view(keys, at, [(0, D_FULL), (KW, B), (1, HD)]),
                        view(keys, at, [(1, D_FULL), (KW, B), (1, HD)]), ALU.mult)
                at = h.slot * LB * B * KW
                nc.gpsimd.tensor_tensor(
                    view(z, h.slot * LB * ZW + PAIRS, [(ZW, LB), (HD // 2, B), (1, HD // 2)]),
                    view(keys, at, [(B * KW, LB), (KW, B), (1, HD // 2)]),
                    view(keys, at + HD // 2, [(B * KW, LB), (KW, B), (1, HD // 2)]), ALU.mult)\
                    .then_inc(z_ready, 1)

            for s in range(2):
                make_z(Turn(0, s))
            nc.gpsimd.memset(ident[:], 0.0).then_inc(pool_const, 1)
            nc.gpsimd.memset(before[:], 1.0).then_inc(pool_const, 1)
            pool.wait_ge(pool_const, 2)
            nc.gpsimd.affine_select(out=ident[:], in_=ident[:], compare_op=ALU.not_equal, fill=1.0,
                                    base=0, pattern=[[-1, P]], channel_multiplier=1)
            nc.gpsimd.affine_select(out=before[:], in_=before[:], compare_op=ALU.is_gt, fill=0.0,
                                    base=0, pattern=[[1, P]], channel_multiplier=-1)
            nc.gpsimd.memset(ones[:], 1.0)
            nc.gpsimd.memset(ones_row[:], 1.0)
            nc.gpsimd.iota(down[:], [[-1, E]], base=E, channel_multiplier=0, allow_small_or_imprecise_dtypes=True)
            nc.gpsimd.iota(fills[:], [[P, H]], base=0, channel_multiplier=0, allow_small_or_imprecise_dtypes=True)
            nc.gpsimd.iota(tile_id[:], [[1, TILES]], base=0, channel_multiplier=0,
                           allow_small_or_imprecise_dtypes=True).then_inc(consts_ready, 1)

            def step(h):
                pool.wait_ge(q_ready, h.n + 1)
                for b in range(LB):
                    pool.wait_ge(y_ready_b, h.n * LB + b + 1)
                    await_count(pool, att_ready_b, (h - 1).n * LB + b + 1)
                    at_y = (h.slot * LB + b) * (D_FULL + 1) * B * YW
                    at_q = (h.slot * LB + b) * B * QW
                    nc.gpsimd.tensor_tensor(
                        view(prods, b * ROWS * HD + D_FULL + 1, [(1, D_FULL - 1), (HD * HD, B), (HD, HD)]),
                        view(y, at_y + B * YW + YPAD - 1, [(B * YW - 1, D_FULL - 1), (YW, B), (1, HD)]),
                        view(queries, at_q + YPAD - 1, [(-1, D_FULL - 1), (QW, B), (1, HD)]),
                        ALU.mult).then_inc(far_done_b, 1)
                if not isinstance(h.n, int) or h.n + 2 < H:
                    make_z(h + 2)

            run_steps(pool, step, 0, H - 1, 2, H - 3)

            pool.wait_ge(rows_zeroed, 16)
            pool.wait_ge(slots_ready, 1)
            for n in range(H):
                pool.wait_ge(rows_ready, n + 1)
                for k in range(TOPK):
                    nc.gpsimd.indirect_dma_start(
                        routed_in, bass.IndirectOffsetOnAxis(ap=slot_of[:, n, k:k + 1].bitcast(U32), axis=0),
                        rows[:, n % ROUND, k], None).then_inc(scattered[n % ROUND], 16)

            for s in range(2):
                pool.wait_ge(r_stored[s], 16 * ((TILES + 1 - s) // 2))
            for s in range(ROUND):
                pool.wait_ge(scattered[s], 16 * TOPK * (H // ROUND))
            for n in range(H):
                await_count(pool, both_ready, n - ROUND + 1)
                for k in range(TOPK):
                    nc.gpsimd.indirect_dma_start(
                        rows[:, n % ROUND, k], None, routed_out,
                        bass.IndirectOffsetOnAxis(ap=slot_of[:, n, k:k + 1].bitcast(U32), axis=0))\
                        .then_inc(gathered[n % ROUND], 16)

        @block.scalar
        def _(act):
            act.dma_start(gates[:, 0:1], g_xattn.partition_broadcast(P)).then_inc(gates_loaded, 16)
            act.dma_start(gates[:, 1:2], g_ffn.partition_broadcast(P)).then_inc(gates_loaded, 16)
            act.dma_start(gate_sb[:], gate_w).then_inc(gatew_loaded, 16)
            act.dma_start(sw13_sb[:], sw13).then_inc(shared_loaded, 16)
            act.dma_start(sw2_sb[:], sw2).then_inc(shared_loaded, 16)
            act.wait_ge(zeros_ready, 1)
            act.dma_start(routed_in.rearrange("(n p) c -> p n c", p=P),
                          view(zeros, 0, [(0, TILES), (1, L)])).then_inc(rows_zeroed, 16)
            act.dma_start(w13_sb[:], w13).then_inc(experts_loaded, 16)
            act.dma_start(w2_sb[:], w2).then_inc(experts_loaded, 16)
            act.wait_ge(gates_loaded, 32)
            nc.scalar.activation(tanh_g[:], gates[:], ACT.Tanh).then_inc(tanh_ready, 1)
            act.wait_ge(eps_ready, 1)
            act.wait_ge(var1_ready, 1)
            nc.scalar.activation(std1[:], var1[:], ACT.Sqrt, bias=eps[:, 0:1]).then_inc(std1_ready, 1)

            def load_queries(h):
                act.wait_ge(q_done, h.n + 1)
                await_count(act, near_done_b, ((h - 2).n + 1) * LB)
                await_count(act, far_done_b, ((h - 2).n + 1) * LB)
                src = q_ps.rearrange("p (r i) -> p r i", i=HD)
                dst = queries[:, h.slot].rearrange("p l (b i) -> p (l b) i", i=QW)
                nc.scalar.activation(dst[:, :, YPAD:YPAD + HD], src, ACT.Copy)
                nc.scalar.activation(dst[:, :, 0:YPAD], src[:, :, HD - YPAD:HD], ACT.Copy)
                nc.scalar.activation(dst[:, :, YPAD + HD:YPAD + HD + D_FULL], src[:, :, 0:D_FULL], ACT.Copy)\
                    .then_inc(q_ready, 1)

            def load_y(h, b):
                act.wait_ge(y_done_b, h.n * LB + b + 1)
                await_count(act, near_done_b, (h - 2).n * LB + b + 1)
                await_count(act, far_done_b, (h - 2).n * LB + b + 1)
                src = y_ps[b][:, :].rearrange("p (r i) -> p r i", i=HD)
                dst = y[:, h.slot, b].rearrange("p (r i) -> p r i", i=YW)
                nc.scalar.activation(dst[:, 0:D_FULL * B, YPAD:YW], src, ACT.Copy)
                nc.scalar.activation(dst[:, B:D_FULL * B, 0:YPAD], src[:, B:D_FULL * B, HD - YPAD:HD], ACT.Copy)
                src4 = y4_ps[b]
                nc.scalar.activation(
                    view(y, ((h.slot * LB + b) * (D_FULL + 1) + D_FULL) * B * YW + YPAD,
                         [(YW, B), (HD // 2, 2), (1, HD // 2)]),
                    bass.AP(src4.tensor, src4.offset, [list(src4.ap[0]), [HD // 2, B], [0, 2], [1, HD // 2]]),
                    ACT.Copy).then_inc(y_ready_b, 1)

            def deviation(h):
                act.wait_ge(mv_ready, h.n + 1)
                await_count(act, rstd_ready, (h - 1).n)
                nc.scalar.activation(mean_all[:, bass.ds(h.n, 1)], mv2[:, h.slot, 0:1], ACT.Copy)
                nc.scalar.activation(std2[:, h.slot:h.slot + 1], mv2[:, h.slot, 1:2], ACT.Sqrt,
                                     bias=eps[:, 0:1]).then_inc(std_ready, 1)

            def load_xnT(h):
                act.wait_ge(xnT_done, h.n + 1)
                await_count(act, gate_done, (h - 1).n)
                src = xnT_ps.rearrange("p (c t) -> p c t", c=LB)
                nc.scalar.activation(xnT[:, h.slot], src, ACT.Copy)
                nc.scalar.activation(xnT_all[:, :, bass.ds(h.n * P, P)], src, ACT.Copy).then_inc(xnT_ready, 1)

            def load_logits(h):
                act.wait_ge(gate_done, h.n + 1)
                nc.scalar.activation(logits[:, bass.ds(h.n * E, E)], gate_ps, ACT.Copy).then_inc(logits_ready, 1)

            def step(h):
                now = h.n if isinstance(h.n, int) else None
                if now is None or now < H:
                    load_y(h, 0)
                    load_y(h, 1)
                if now is None or now + 1 < H:
                    load_queries(h + 1)
                if now is None or 1 <= now <= H:
                    deviation(h - 1)
                if now is None or 3 <= now:
                    load_logits(h - 3)
                if now is None or 2 <= now <= H + 1:
                    load_xnT(h - 2)

            load_queries(Turn(0, 0))
            run_steps(act, step, 0, H + 2, 4, H - 3)

            act.wait_ge(logits_ready, H)
            nc.scalar.activation(probs[:].rearrange("p h e -> p (h e)"), logits[:], ACT.Sigmoid)\
                .then_inc(probs_ready, 1)
            for c in range(NCHUNK):
                act.wait_ge(up_done, c + 1)
                await_count(act, sh_ready, c - 1)
                nc.scalar.activation(shared_act[:, c % 2], up_ps[c % 2][0][:, :], ACT.Silu)\
                    .then_inc(sact_ready, 1)

            def routed(t):
                now = t.n if isinstance(t.n, int) else None
                if now is None or now < TILES:
                    act.wait_ge(rT_done, t.n + 1)
                    await_count(act, ru_done, (t - 1).n)
                    nc.scalar.activation(r_inT[:, t.slot], rT_ps[t.slot].rearrange("p (c t) -> p c t", c=LB),
                                         ACT.Copy).then_inc(rT_ready, 1)
                if now is None or 1 <= now <= TILES:
                    u = t - 1
                    act.wait_ge(ru_done, u.n + 1)
                    await_count(act, rh_ready, (u - 1).n)
                    nc.scalar.activation(r_act[:, u.slot], ru_ps[u.slot][:, 0:HID], ACT.Silu)\
                        .then_inc(ract_ready, 1)
                if now is None or now >= 3:
                    v = t - 3
                    act.wait_ge(ro_done, v.n + 1)
                    if now is None or now >= 5:
                        act.wait_ge(r_stored[v.slot], v.i * 16)
                    nc.scalar.activation(r_out[:, v.slot], ro_ps[v.slot], ACT.Copy).then_inc(ro_ready, 1)

            run_steps(act, routed, 0, TILES + 2, 6, TILES - 2)

        @block.vector
        def _(dve):
            nc.vector.memset(zeros[:], 0.0).then_inc(zeros_ready, 1)
            nc.vector.memset(eps[:], EPS).then_inc(eps_ready, 1)
            nc.vector.memset(filt[:, 0:P - 1], 0.0)
            nc.vector.memset(filt[:, P - 1 + L:KPAD], 0.0).then_inc(filt_zeroed, 1)
            dve.wait_ge(small_loaded, 32)
            dve.wait_ge(filt_zeroed, 1)
            nc.vector.tensor_tensor(filt[:, P - 1:P], filt[:, P - 1:P], skip_sb[:, :], ALU.add)\
                .then_inc(filt_ready, 1)

            for h in range(H):
                if h % 4 == 0:
                    dve.wait_ge(x_loaded[h // 4], 16)
                last = nc.vector.bn_stats(st1[:, h, :], x_all[:, h * L:(h + 1) * L])
            last.then_inc(norm1, 1)
            dve.wait_ge(norm1, 1)
            me, mo = st1[:, :, 1], st1[:, :, 4]
            nc.vector.tensor_tensor(mean1[:], me, mo, ALU.add)
            nc.vector.tensor_tensor(half1[:], me, mo, ALU.subtract)
            nc.vector.tensor_tensor(var1[:], st1[:, :, 2], st1[:, :, 5], ALU.add).then_inc(norm1, 1)
            dve.wait_ge(norm1, 2)
            nc.vector.tensor_scalar(mean1[:], mean1[:], 0.5, None, ALU.mult)
            nc.vector.tensor_scalar(var1[:], var1[:], 1.0 / L, None, ALU.mult)
            nc.vector.scalar_tensor_tensor(rstd1[:], half1[:], 0.25, half1[:], ALU.mult, ALU.mult)\
                .then_inc(norm1, 1)
            dve.wait_ge(norm1, 3)
            nc.vector.tensor_tensor(var1[:], var1[:], rstd1[:], ALU.add).then_inc(var1_ready, 1)
            dve.wait_ge(std1_ready, 1)
            nc.vector.reciprocal(rstd1[:], std1[:]).then_inc(norm1, 1)
            dve.wait_ge(norm1, 4)

            def norm_x(h):
                await_count(dve, q_done, (h - 1).n)
                nc.vector.tensor_scalar(xq[:, h.slot], head_rows(x_all, h.n), mean1[:, bass.ds(h.n, 1)],
                                        rstd1[:, bass.ds(h.n, 1)], ALU.subtract, ALU.mult)\
                    .then_inc(xq_ready, 1)

            def attend(h, b):
                dve.wait_ge(y_ready_b, h.n * LB + b + 1)
                await_count(dve, att_ready_b, (h - 1).n * LB + b + 1)
                at_y = (h.slot * LB + b) * (D_FULL + 1) * B * YW
                at_q = (h.slot * LB + b) * B * QW
                nc.vector.tensor_tensor(
                    view(prods, b * ROWS * HD, [(1, D_FULL + 1), (HD * HD, B), (HD, HD)]),
                    view(y, at_y + YPAD, [(B * YW, D_FULL + 1), (YW, B), (1, HD)]),
                    view(queries, at_q + YPAD, [(1, D_FULL + 1), (QW, B), (1, HD)]),
                    ALU.mult).then_inc(near_done_b, 1)
                dve.wait_ge(near_done_b, h.n * LB + b + 1)
                dve.wait_ge(far_done_b, h.n * LB + b + 1)
                if b == 0:
                    await_count(dve, att_done, (h - 1).n)
                nc.vector.tensor_reduce(att[:, h.slot, b], prods[:, b].rearrange("p (r t) -> p r t", t=HD),
                                        AX_X, ALU.add).then_inc(att_ready_b, 1)

            def add_attention(h):
                await_count(dve, std_ready, (h - 1).n)
                dve.wait_ge(att_done, h.n + 1)
                nc.vector.scalar_tensor_tensor(head_rows(x_all, h.n), att_ps, tanh_g[:, 0:1],
                                               head_rows(x_all, h.n), ALU.mult, ALU.add).then_inc(x1_ready, 1)
                dve.drain()
                nc.vector.bn_stats(st2[:, h.slot], head_rows(x_all, h.n))
                dve.drain()
                nc.vector.bn_aggr(mv2[:, h.slot], st2[:, h.slot]).then_inc(mv_ready, 1)

            def norm_x1(h):
                dve.wait_ge(std_ready, h.n + 1)
                nc.vector.reciprocal(rstd_all[:, bass.ds(h.n, 1)], std2[:, h.slot:h.slot + 1])\
                    .then_inc(rstd_ready, 1)
                dve.wait_ge(rstd_ready, h.n + 1)
                await_count(dve, xnT_done, (h - 1).n)
                nc.vector.tensor_scalar(xn[:, h.slot], head_rows(x_all, h.n), mean_all[:, bass.ds(h.n, 1)],
                                        rstd_all[:, bass.ds(h.n, 1)], ALU.subtract, ALU.mult)\
                    .then_inc(xn_ready, 1)

            def step(h):
                now = h.n if isinstance(h.n, int) else None
                if now is None or now < H:
                    dve.wait_ge(q_ready, h.n + 1)
                    attend(h, 0)
                if now is None or now >= 1:
                    add_attention(h - 1)
                if now is None or now < H:
                    attend(h, 1)
                if now is None or now + 2 < H:
                    norm_x(h + 2)
                if now is None or now >= 1:
                    norm_x1(h - 1)

            norm_x(Turn(0, 0))
            norm_x(Turn(0, 1))
            dve.wait_ge(tanh_ready, 1)
            run_steps(dve, step, 0, H, 4, H - 3)

            steps = [0]

            def link(ins):
                steps[0] += 1
                ins.then_inc(route, 1)
                dve.wait_ge(route, steps[0])

            dve.wait_ge(probs_ready, 1)
            dve.wait_ge(consts_ready, 1)
            down_b = view(down, 0, [(0, H), (1, E)])

            def best(of, k):
                top = score[:, :, k:k + 1].broadcast_to([P, H, E])
                link(nc.vector.tensor_reduce(score[:, :, k], of[:], AX_X, ALU.max))
                link(nc.vector.tensor_tensor(is_max[:], of[:], top, ALU.is_equal))
                link(nc.vector.tensor_tensor(rank[:], is_max[:], down_b, ALU.mult))
                link(nc.vector.tensor_reduce(top_rank[:, :, k], rank[:], AX_X, ALU.max))
                link(nc.vector.tensor_tensor(chosen[:, k], down_b,
                                             top_rank[:, :, k:k + 1].broadcast_to([P, H, E]), ALU.is_equal))

            best(probs, 0)
            link(nc.vector.scalar_tensor_tensor(rest[:], chosen[:, 0], -2.0, probs[:], ALU.mult, ALU.add))
            best(rest, 1)
            nc.vector.tensor_tensor(mask[:].rearrange("p (h e) -> p h e", h=H), chosen[:, 0], chosen[:, 1],
                                    ALU.add).then_inc(mask_ready, 1)

            dve.wait_ge(place_done, 1)
            link(nc.vector.tensor_reduce(count[:], total_ps.rearrange("p (h e) -> p e h", h=H), AX_X, ALU.add))
            link(nc.vector.tensor_tensor(over[:], view(count, 0, [(1, E), (0, H)]), view(fills, 0, [(0, E), (1, H)]),
                                         ALU.is_gt))
            link(nc.vector.tensor_reduce(tiles[:], over[:], AX_X, ALU.add))
            link(nc.vector.tensor_tensor_scan(tiles_to[:], ones_row[:], tiles[:], 0.0, ALU.mult, ALU.add))
            link(nc.vector.tensor_tensor(tiles_before[:], tiles_to[:], tiles[:], ALU.subtract))
            link(nc.vector.scalar_tensor_tensor(place[:], view(tiles_before, 0, [(0, H), (1, E)]), float(P),
                                                place_ps.rearrange("p (h e) -> p h e", h=H), ALU.mult, ALU.add))
            for k in range(TOPK):
                last = nc.vector.tensor_tensor(picked[:, k], chosen[:, k], place[:], ALU.mult)
            link(last)
            for k in range(TOPK):
                last = nc.vector.tensor_reduce(slot_f[:, :, k], picked[:, k], AX_X, ALU.add)
            link(last)
            nc.vector.tensor_copy(slot_of[:], slot_f[:]).then_inc(slots_ready, 1)
            link(nc.vector.tensor_tensor(
                ended[:], bass.AP(tiles_to[:].tensor, tiles_to[:].offset, [list(tiles_to[0:1].ap[0]), [0, TILES], [1, E]]),
                bass.AP(tile_id[:].tensor, tile_id[:].offset, [list(tile_id[0:1].ap[0]), [1, TILES], [0, E]]),
                ALU.is_le))
            link(nc.vector.tensor_reduce(tile_expert_f[:], ended[:], AX_X, ALU.add))
            nc.vector.tensor_scalar(tile_expert[:], tile_expert_f[:], float(E - 1), None, ALU.min)\
                .then_inc(table_ready, 1)

            for c in range(NCHUNK):
                dve.wait_ge(sact_ready, c + 1)
                await_count(dve, sout_done, CHUNK * (c - 1))
                nc.vector.tensor_tensor(shared_h[:, c % 2], shared_act[:, c % 2], up_ps[c % 2][1][:, :], ALU.mult)\
                    .then_inc(sh_ready, 1)
                for n in range(CHUNK * c, CHUNK * c + CHUNK):
                    await_count(dve, rows_ready, n - 1)
                    nc.vector.tensor_scalar(xn_again[:, n % 2], x_all[:, n * L:(n + 1) * L], mean_all[:, n:n + 1],
                                            rstd_all[:, n:n + 1], ALU.subtract, ALU.mult)\
                        .then_inc(again_ready, 1)
                    dve.wait_ge(again_ready, n + 1)
                    await_count(dve, scattered[n % ROUND], 16 * TOPK * (n // ROUND))
                    for k in range(TOPK):
                        last = nc.vector.tensor_scalar(rows[:, n % ROUND, k], xn_again[:, n % 2],
                                                       score[:, n, k:k + 1], None, ALU.mult)
                    last.then_inc(rows_ready, 1)
                for n in range(CHUNK * c, CHUNK * c + CHUNK):
                    dve.wait_ge(sout_done, n + 1)
                    nc.vector.scalar_tensor_tensor(base_all[:, n * L:(n + 1) * L], sh_ps[n % CHUNK], tanh_g[:, 1:2],
                                                   x_all[:, n * L:(n + 1) * L], ALU.mult, ALU.add)\
                        .then_inc(base_ready, 1)

            def routed(t):
                now = t.n if isinstance(t.n, int) else None
                if now is None or 2 <= now <= TILES + 1:
                    w = t - 2
                    dve.wait_ge(rhT_done, w.n + 1)
                    await_count(dve, ro_done, (w - 1).n)
                    nc.vector.tensor_copy(r_hT[:, w.slot], rh_ps[w.slot]).then_inc(rhT_ready, 1)
                if now is None or 1 <= now <= TILES:
                    u = t - 1
                    dve.wait_ge(ract_ready, u.n + 1)
                    await_count(dve, rhT_done, (u - 1).n)
                    nc.vector.tensor_tensor(r_h[:, u.slot], r_act[:, u.slot], ru_ps[u.slot][:, HID:2 * HID],
                                            ALU.mult).then_inc(rh_ready, 1)

            run_steps(dve, routed, 0, TILES + 1, 4, TILES - 2)

            dve.wait_ge(base_ready, H)
            for n in range(H):
                dve.wait_ge(gathered[n % ROUND], 16 * TOPK * (n // ROUND + 1))
                nc.vector.tensor_tensor(both[:, n % 2], rows[:, n % ROUND, 0], rows[:, n % ROUND, 1], ALU.add)\
                    .then_inc(both_ready, 1)
                dve.wait_ge(both_ready, n + 1)
                await_count(dve, out_stored[n % ROUND], 16 * (n // ROUND))
                nc.vector.scalar_tensor_tensor(result[:, n % ROUND], both[:, n % 2], tanh_g[:, 1:2],
                                               base_all[:, n * L:(n + 1) * L], ALU.mult, ALU.add)\
                    .then_inc(result_ready, 1)
                dve.wait_ge(result_ready, n + 1)

        @block.tensor
        def _(pe):
            def transpose_q(h):
                pe.wait_ge(xq_ready, h.n + 1)
                await_count(pe, q_ready, h.n)
                for b in range(LB):
                    last = nc.tensor.transpose(q_ps[:, b * P:(b + 1) * P],
                                               xq[:, h.slot, b * P:(b + 1) * P], ident[:])
                last.then_inc(q_done, 1)

            def convolve(h):
                pe.wait_ge(toep_loaded[h.slot], h.i * 16 + 16)
                pe.wait_ge(z_ready, h.n + 1)
                near, far = toep[:, h.slot, 0:P], toep[:, h.slot, P:2 * P]
                for b, terms in enumerate([[(near, 0)], [(far, 0), (near, 1)]]):
                    await_count(pe, y_ready_b, (h - 1).n * LB + b + 1)
                    for n, (w, m) in enumerate(terms):
                        nc.tensor.matmul(y_ps[b][:, :], w, z[:, h.slot, m, 0:PAIRS],
                                         start=(n == 0), stop=(n == len(terms) - 1))
                    for n, (w, m) in enumerate(terms):
                        last = nc.tensor.matmul(y4_ps[b], w, z[:, h.slot, m, PAIRS:ZW],
                                                start=(n == 0), stop=(n == len(terms) - 1))
                    last.then_inc(y_done_b, 1)

            def transpose_att(h):
                pe.wait_ge(att_ready_b, (h.n + 1) * LB)
                await_count(pe, x1_ready, h.n)
                for b in range(LB):
                    last = nc.tensor.transpose(att_ps[:, b * P:(b + 1) * P], att[:, h.slot, b], ident[:])
                last.then_inc(att_done, 1)

            def transpose_xn(h):
                pe.wait_ge(xn_ready, h.n + 1)
                await_count(pe, xnT_ready, h.n)
                for b in range(LB):
                    last = nc.tensor.transpose(xnT_ps[:, b * P:(b + 1) * P], xn[:, h.slot, b * P:(b + 1) * P],
                                               ident[:])
                last.then_inc(xnT_done, 1)

            def gate(h):
                pe.wait_ge(xnT_ready, h.n + 1)
                await_count(pe, logits_ready, h.n)
                for b in range(LB):
                    last = nc.tensor.matmul(gate_ps, xnT[:, h.slot, b], gate_sb[:, b], start=(b == 0),
                                            stop=(b == LB - 1))
                last.then_inc(gate_done, 1)

            def step(h):
                now = h.n if isinstance(h.n, int) else None
                if now is None or now < H:
                    convolve(h)
                if now is None or now + 1 < H:
                    transpose_q(h + 1)
                if now is None or 1 <= now <= H:
                    transpose_att(h - 1)
                if now is None or now >= 3:
                    gate(h - 3)
                if now is None or 2 <= now <= H + 1:
                    transpose_xn(h - 2)

            pe.wait_ge(consts_ready, 1)
            pe.wait_ge(gatew_loaded, 16)
            transpose_q(Turn(0, 0))
            run_steps(pe, step, 0, H + 2, 4, H - 3)

            pe.wait_ge(shared_loaded, 32)
            pe.wait_ge(xnT_ready, H)
            pe.wait_ge(y_ready_b, H * LB)

            def up(c):
                await_count(pe, sh_ready, c - 1)
                for j in range(2):
                    for b in range(LB):
                        last = nc.tensor.matmul(up_ps[c % 2][j][:, :], sw13_sb[:, b, j * HID:(j + 1) * HID],
                                                xnT_all[:, b, c * CHUNK * P:(c + 1) * CHUNK * P],
                                                start=(b == 0), stop=(b == LB - 1))
                last.then_inc(up_done, 1)

            def count_rows():
                pe.wait_ge(mask_ready, 1)
                nc.tensor.matmul(place_ps, before[:], mask[:], start=True, stop=False)
                for h in range(H - 1):
                    nc.tensor.matmul(place_ps[:, (h + 1) * E:H * E], ones[:],
                                     view(mask, h * E, [(0, H - 1 - h), (1, E)]),
                                     start=False, stop=(h == H - 2))
                nc.tensor.matmul(total_ps, ones[:], mask[:], start=True, stop=True).then_inc(place_done, 1)

            up(0)
            up(1)
            count_rows()
            pe.wait_ge(x1_ready, H)
            for c in range(NCHUNK):
                pe.wait_ge(sh_ready, c + 1)
                await_count(pe, base_ready, CHUNK * c)
                for t in range(CHUNK):
                    nc.tensor.matmul(sh_ps[t], shared_h[:, c % 2, t * P:(t + 1) * P], sw2_sb[:], start=True,
                                     stop=True).then_inc(sout_done, 1)
                if c + 2 < NCHUNK:
                    up(c + 2)

            pe.wait_ge(experts_loaded, 32)
            pe.wait_ge(table_ready, 1)
            pe.wait_ge(base_ready, H)
            pe.wait_ge(sh_ready, NCHUNK)

            def expert_of(t):
                return pe.value_load(tile_expert[0:1, bass.ds(t.n, 1)], min_val=0, max_val=E - 1)

            def routed(t):
                now = t.n if isinstance(t.n, int) else None
                if now is None or now < TILES:
                    pe.wait_ge(r_loaded[t.slot], t.i * 16 + 16)
                    await_count(pe, rT_ready, (t - 1).n)
                    for b in range(LB):
                        last = nc.tensor.transpose(rT_ps[t.slot][:, b * P:(b + 1) * P],
                                                   r_in[:, t.slot, b * P:(b + 1) * P], ident[:])
                    last.then_inc(rT_done, 1)
                if now is None or 1 <= now <= TILES:
                    u = t - 1
                    e = expert_of(u)
                    pe.wait_ge(rT_ready, u.n + 1)
                    await_count(pe, rh_ready, (u - 1).n)
                    for b in range(LB):
                        last = nc.tensor.matmul(ru_ps[u.slot], r_inT[:, u.slot, b],
                                                w13_sb[:, b, bass.ds(e * (2 * HID), 2 * HID)],
                                                start=(b == 0), stop=(b == LB - 1))
                    last.then_inc(ru_done, 1)
                if now is None or now >= 3:
                    v = t - 3
                    e = expert_of(v)
                    pe.wait_ge(rhT_ready, v.n + 1)
                    await_count(pe, ro_ready, (v - 1).n)
                    nc.tensor.matmul(ro_ps[v.slot], r_hT[:, v.slot], w2_sb[:, bass.ds(e * L, L)],
                                     start=True, stop=True).then_inc(ro_done, 1)
                if now is None or 2 <= now <= TILES + 1:
                    w = t - 2
                    pe.wait_ge(rh_ready, w.n + 1)
                    await_count(pe, rhT_ready, (w - 1).n)
                    nc.tensor.transpose(rh_ps[w.slot], r_h[:, w.slot], ident[:]).then_inc(rhT_done, 1)

            run_steps(pe, routed, 0, TILES + 2, 4, TILES - 2)


def kernel(x, ctx_2048, g_xattn, g_ffn, L0_xattn_ssm_kernel, L0_xattn_D, L0_ffn_gate_w, L0_ffn_w1, L0_ffn_w2,
           L0_ffn_w3, L0_ffn_sw1, L0_ffn_sw2, L0_ffn_sw3):
    import numpy as np
    import concourse.bacc as bacc
    from concourse.bass_utils import run_bass_kernel_spmd

    def kmajor(w):
        return w.T.reshape(LB, P, -1).transpose(1, 0, 2)

    xs = x.reshape(B, H, HD, L).transpose(0, 2, 1, 3).reshape(P, H * L)
    c = ctx_2048.reshape(B, H, HD, LB, P)[..., ::-1].transpose(1, 4, 3, 0, 2)
    c = np.concatenate([c, c[..., :D_FULL]], axis=-1).reshape(H, P, LB, B * KW)
    w13 = np.stack([np.concatenate([kmajor(L0_ffn_w1[e]), kmajor(L0_ffn_w3[e])], axis=-1) for e in range(E)], axis=2)
    arrays = {
        "x": xs,
        "ctx": c,
        "g_xattn": g_xattn,
        "g_ffn": g_ffn,
        "taps": L0_xattn_ssm_kernel,
        "skip": L0_xattn_D.reshape(H, 1),
        "gate_w": kmajor(L0_ffn_gate_w),
        "w13": w13.reshape(P, LB, E * 2 * HID),
        "w2": L0_ffn_w2.transpose(2, 0, 1).reshape(HID, E * L),
        "sw13": np.concatenate([kmajor(L0_ffn_sw1), kmajor(L0_ffn_sw3)], axis=-1),
        "sw2": L0_ffn_sw2.T,
    }
    arrays = {name: np.ascontiguousarray(a) for name, a in arrays.items()}
    nc = bacc.Bacc("TRN2", target_bir_lowering=False, num_devices=1)
    aps = [nc.dram_tensor(f"in_{name}", a.shape, mybir.dt.from_np(a.dtype), kind="ExternalInput").ap()
           for name, a in arrays.items()]
    out = nc.dram_tensor("out", [P, H * L], F32, kind="ExternalOutput").ap()
    flamingo_block(nc, *aps, out)
    done = run_bass_kernel_spmd(nc, [{f"in_{name}": a for name, a in arrays.items()}], core_ids=[0])
    got = done.results[0]["out"]
    return np.ascontiguousarray(got.reshape(B, HD, H, L).transpose(0, 2, 1, 3).reshape(B, H * HD, L))
```

```python
from contextlib import ExitStack

import concourse.bass as bass
from concourse import mybir

ALU = mybir.AluOpType
ACT = mybir.ActivationFunctionType
F32 = mybir.dt.float32
BF16 = mybir.dt.bfloat16
I32 = mybir.dt.int32
U32 = mybir.dt.uint32
AX_X = mybir.AxisListType.X

P = 128
H = 16
B = 16
HD = 8
L = 256
LB = L // P
E = 8
TOPK = 2
HID = 128
EPS = 1e-5

D_FULL = HD // 2
PAIRS = D_FULL * B * HD
PAIRS4 = B * HD // 2
ZW = PAIRS + PAIRS4
KW = HD + D_FULL
YW = HD + D_FULL - 1
YPAD = D_FULL - 1
QW = 16
ROWS = B * HD

CHUNK = 4
NCHUNK = H // CHUNK
SLOTS = H * ROWS * TOPK
TILES = SLOTS // P + E - 1
KPAD = 384
ROUND = 4
RW = L + 4
SPARE = 4
TILES_UP = -(-TILES // SPARE) * SPARE
KR = 4
RR = 8


def await_count(eng, sem, n):
    if n > 0:
        eng.wait_ge(sem, n)


def view(tensor, offset, dims):
    whole = tensor[:]
    return bass.AP(whole.tensor, offset + whole.offset, [list(whole.ap[0])] + [list(d) for d in dims])


def flamingo_block(nc, x, ctx, g_xattn, g_ffn, taps, skip, gate_w, w13, w2, sw13, sw2, out):
    filt_dram = nc.dram_tensor("filt_dram", [H, KPAD], F32, kind="Internal").ap()
    routed_in = nc.dram_tensor("routed_in", [TILES_UP * P, RW], F32, kind="Internal").ap()
    routed_out = nc.dram_tensor("routed_out", [SLOTS + SPARE * P, L], F32, kind="Internal").ap()

    with ExitStack() as stack:
        def sb(name, shape, dt=F32):
            return stack.enter_context(nc.sbuf_tensor(name, shape, dt))

        def sem(name):
            return stack.enter_context(nc.semaphore(name))

        ident = sb("ident", [P, P])
        before = sb("before", [P, P], BF16)
        ones = sb("ones", [P, P], BF16)
        ones_row = sb("ones_row", [P, E])
        down = sb("down", [P, E])
        fills = sb("fills", [P, H])
        tile_id = sb("tile_id", [P, TILES])
        row_id = sb("row_id", [P, H, TOPK], I32)
        empty = sb("empty", [P, SPARE, RW])
        eps = sb("eps", [P, 1])
        gates = sb("gates", [P, 2])
        tanh_g = sb("tanh_g", [P, 2])
        filt = sb("filt", [H, KPAD])
        skip_sb = sb("skip_sb", [H, 1])
        gate_sb = sb("gate_sb", [P, LB, E])
        w13_sb = sb("w13_sb", [P, LB, E * 2 * HID])
        w2_sb = sb("w2_sb", [P, E * L])
        sw13_sb = sb("sw13_sb", [P, LB, 2 * HID])
        sw2_sb = sb("sw2_sb", [P, L])
        x_all = sb("x_all", [P, H, L])
        xn_all = sb("xn_all", [P, H, L])
        xnT_all = sb("xnT_all", [P, LB, H * P])
        st1 = sb("st1", [P, H, 6])
        sum1 = sb("sum1", [P, H])
        var1 = sb("var1", [P, H])
        half1 = sb("half1", [P, H])
        std1 = sb("std1", [P, H])
        rstd1 = sb("rstd1", [P, H])
        shift1 = sb("shift1", [P, H])
        keys = sb("keys", [P, KR, LB, B * KW])
        toep = sb("toep", [P, KR, L])
        z = sb("z", [P, 2, LB, ZW])
        xq = sb("xq", [P, 2, L])
        queries = sb("queries", [P, 2, LB, B * QW])
        y = sb("y", [P, 2, LB, (D_FULL + 1) * B * YW])
        prods = sb("prods", [P, LB, ROWS * HD])
        att = sb("att", [P, 2, LB, ROWS])
        st2 = sb("st2", [P, 2, 6])
        mv2 = sb("mv2", [P, 2, 2])
        std2 = sb("std2", [P, 2])
        rstd2 = sb("rstd2", [P, 2])
        shift2 = sb("shift2", [P, 2])
        logits = sb("logits", [P, H, E])
        probs = sb("probs", [P, H, E])
        score = sb("score", [P, H, TOPK])
        is_max = sb("is_max", [P, H, E])
        rank = sb("rank", [P, H, E])
        top_rank = sb("top_rank", [P, H, TOPK])
        chosen = sb("chosen", [P, TOPK, H, E])
        rest = sb("rest", [P, H, E])
        mask = sb("mask", [P, H * E], BF16)
        count = sb("count", [P, E])
        over = sb("over", [P, E, H])
        tiles = sb("tiles", [P, E])
        tiles_to = sb("tiles_to", [P, E])
        tiles_before = sb("tiles_before", [P, E])
        place = sb("place", [P, H, E])
        picked = sb("picked", [P, TOPK, H, E])
        slot_f = sb("slot_f", [P, TOPK, H])
        slot_of = sb("slot_of", [P, TOPK, H], I32)
        ended = sb("ended", [1, TILES, E])
        tile_expert_f = sb("tile_expert_f", [1, TILES])
        tile_expert = sb("tile_expert", [1, TILES], I32)
        rows = sb("rows", [P, ROUND, TOPK, RW])
        shared_act = sb("shared_act", [P, 2, CHUNK * P])
        shared_h = sb("shared_h", [P, 2, CHUNK * P])
        r_in = sb("r_in", [P, RR, RW])
        r_inT = sb("r_inT", [P, 2, LB, P])
        r_act = sb("r_act", [P, 2, HID])
        r_h = sb("r_h", [P, 2, HID])
        r_hT = sb("r_hT", [P, 2, P])
        r_out = sb("r_out", [P, RR, L])
        results = sb("results", [P, ROUND, TOPK, L])
        both = sb("both", [P, 2, L])
        final = sb("final", [P, ROUND, L])

        banks = [stack.enter_context(nc.psum_tensor(f"bank{n}", [P, 512], F32)) for n in range(8)]
        y_ps = [banks[0], banks[1]]
        y4_ps = [banks[2][:, 0:PAIRS4], banks[3][:, 0:PAIRS4]]
        q_ps = banks[4][:, 0:L]
        att_ps = banks[5][:, 0:L]
        xnT_ps = banks[6][:, 0:L]
        gate_ps = banks[7][:, 0:E]
        place_ps = banks[4][:, 0:H * E]
        total_ps = banks[4][:, 256:256 + H * E]
        up_ps = [[banks[0], banks[1]], [banks[2], banks[3]]]
        sh_ps = [banks[4 + t][:, 0:L] for t in range(CHUNK)]
        rT_ps = [banks[0 + s][:, 0:256] for s in range(2)]
        ru_ps = [banks[2 + s][:, 0:256] for s in range(2)]
        rh_ps = [banks[4 + s][:, 0:P] for s in range(2)]
        ro_ps = [banks[6 + s][:, 0:256] for s in range(2)]

        x_loaded = [sem(f"x_loaded{c}") for c in range(4)]
        taps_loaded = sem("taps_loaded")
        gates_loaded = sem("gates_loaded")
        gatew_loaded = sem("gatew_loaded")
        shared_loaded = sem("shared_loaded")
        experts_loaded = sem("experts_loaded")
        filt_zeroed = sem("filt_zeroed")
        filt_ready = sem("filt_ready")
        filt_stored = sem("filt_stored")
        keys_loaded = [sem(f"keys_loaded{s}") for s in range(KR)]
        toep_loaded = [sem(f"toep_loaded{s}") for s in range(KR)]
        empty_cleared = sem("empty_cleared")
        empty_ready = sem("empty_ready")
        rows_emptied = sem("rows_emptied")
        masks_set = sem("masks_set")
        ident_ready = sem("ident_ready")
        consts_ready = sem("consts_ready")
        eps_ready = sem("eps_ready")
        tanh_ready = sem("tanh_ready")
        norm1 = sem("norm1")
        var1_ready = sem("var1_ready")
        std1_ready = sem("std1_ready")
        shift1_ready = sem("shift1_ready")
        z_ready = sem("z_ready")
        y_done_b = sem("y_done_b")
        y_ready_b = sem("y_ready_b")
        near_done_b = sem("near_done_b")
        far_done_b = sem("far_done_b")
        att_ready_b = sem("att_ready_b")
        xq_ready = sem("xq_ready")
        q_done = sem("q_done")
        q_ready = sem("q_ready")
        att_done = sem("att_done")
        x1_ready = sem("x1_ready")
        stats_ready = sem("stats_ready")
        mv_ready = sem("mv_ready")
        std_ready = sem("std_ready")
        rstd_ready = sem("rstd_ready")
        shift_ready = sem("shift_ready")
        xn_ready = sem("xn_ready")
        xnT_done = sem("xnT_done")
        xnT_ready = sem("xnT_ready")
        gate_done = sem("gate_done")
        logits_ready = sem("logits_ready")
        probs_ready = sem("probs_ready")
        route = sem("route")
        mask_ready = sem("mask_ready")
        place_done = sem("place_done")
        slots_ready = sem("slots_ready")
        table_ready = sem("table_ready")
        up_done = sem("up_done")
        sact_ready = sem("sact_ready")
        sh_ready = sem("sh_ready")
        sout_done = sem("sout_done")
        base_ready = sem("base_ready")
        rows_ready = sem("rows_ready")
        scattered = [sem(f"scattered{s}") for s in range(ROUND)]
        r_loaded = [sem(f"r_loaded{s}") for s in range(RR)]
        rT_done = sem("rT_done")
        rT_ready = sem("rT_ready")
        ru_done = sem("ru_done")
        ract_ready = sem("ract_ready")
        rh_ready = sem("rh_ready")
        rhT_done = sem("rhT_done")
        rhT_ready = sem("rhT_ready")
        ro_done = sem("ro_done")
        ro_ready = sem("ro_ready")
        r_stored = [sem(f"r_stored{s}") for s in range(RR)]
        results_loaded = [sem(f"results_loaded{s}") for s in range(ROUND)]
        both_ready = sem("both_ready")
        final_ready = sem("final_ready")
        out_stored = [sem(f"out_stored{s}") for s in range(ROUND)]

        block = stack.enter_context(nc.Block())

        @block.sync
        def _(sp):
            def load_keys(h):
                await_count(sp, z_ready, h - KR + 1)
                sp.dma_start(keys[:, h % KR], ctx[h]).then_inc(keys_loaded[h % KR], 16)

            def load_toep(h):
                await_count(sp, y_done_b, (h - KR + 1) * LB)
                src = bass.AP(filt_dram.tensor, h * KPAD, [[1, P], [1, L]])
                sp.dma_start(toep[:, h % KR], src).then_inc(toep_loaded[h % KR], 16)

            load_keys(0)
            sp.dma_start(x_all[:, 0:CHUNK], x[:, 0:CHUNK]).then_inc(x_loaded[0], 16)
            sp.wait_ge(filt_ready, 1)
            sp.dma_start(filt_dram, filt[:, :]).then_inc(filt_stored, 16)
            load_keys(1)
            sp.wait_ge(filt_stored, 16)
            load_toep(0)
            load_toep(1)
            for c in range(1, 4):
                sp.dma_start(x_all[:, CHUNK * c:CHUNK * (c + 1)], x[:, CHUNK * c:CHUNK * (c + 1)])\
                    .then_inc(x_loaded[c], 16)
                if c < 3:
                    load_keys(c + 1)
                    load_toep(c + 1)
            sp.dma_start(gate_sb[:], gate_w).then_inc(gatew_loaded, 16)
            sp.wait_ge(empty_ready, 1)
            for h in range(KR, H):
                load_keys(h)
                load_toep(h)
                if h == KR:
                    sp.dma_start(routed_in.rearrange("(n p s) c -> p n (s c)", p=P, s=SPARE),
                                 view(empty, 0, [(0, TILES_UP // SPARE), (1, SPARE * RW)])).then_inc(rows_emptied, 16)
                if h == KR + 2:
                    sp.dma_start(sw13_sb[:], sw13).then_inc(shared_loaded, 16)
                    sp.dma_start(sw2_sb[:], sw2).then_inc(shared_loaded, 16)
                if h == KR + 4:
                    sp.dma_start(w13_sb[:], w13).then_inc(experts_loaded, 16)
                    sp.dma_start(w2_sb[:], w2).then_inc(experts_loaded, 16)

            for s in range(ROUND):
                sp.wait_ge(scattered[s], 16 * TOPK * (H // ROUND))
            for t in range(TILES):
                if t >= RR:
                    sp.wait_ge(rT_done, t - RR + 1)
                    sp.wait_ge(r_stored[t % RR], 16 * (t // RR))
                sp.dma_start(r_in[:, t % RR], routed_in[t * P:(t + 1) * P, :]).then_inc(r_loaded[t % RR], 16)

            for s in range(RR):
                sp.wait_ge(r_stored[s], 16 * ((TILES - 1 - s) // RR + 1))

            def load_results(h):
                await_count(sp, both_ready, h - ROUND + 1)
                sp.dma_start(results[:, h % ROUND],
                             routed_out[0:SLOTS].rearrange("(k h p) c -> h p k c", k=TOPK, h=H)[h])\
                    .then_inc(results_loaded[h % ROUND], 16)

            for h in range(H):
                load_results(h)
            for s in range(ROUND):
                sp.wait_ge(out_stored[s], 16 * (H // ROUND))

        @block.gpsimd
        def _(pool):
            nc.gpsimd.memset(ident[:], 0.0).then_inc(masks_set, 1)
            pool.wait_ge(masks_set, 1)
            nc.gpsimd.affine_select(out=ident[:], in_=ident[:], compare_op=ALU.not_equal, fill=1.0,
                                    base=0, pattern=[[-1, P]], channel_multiplier=1).then_inc(ident_ready, 1)

            def make_z(h):
                pool.wait_ge(keys_loaded[h % KR], 16 * (h // KR + 1))
                await_count(pool, y_done_b, (h - 1) * LB)
                for b in range(LB):
                    at = (h % KR * LB + b) * B * KW
                    nc.gpsimd.tensor_tensor(
                        z[:, h % 2, b, 0:PAIRS].rearrange("p (d b i) -> p d b i", d=D_FULL, b=B),
                        view(keys, at, [(0, D_FULL), (KW, B), (1, HD)]),
                        view(keys, at, [(1, D_FULL), (KW, B), (1, HD)]), ALU.mult)
                at = h % KR * LB * B * KW
                nc.gpsimd.tensor_tensor(
                    view(z, h % 2 * LB * ZW + PAIRS, [(ZW, LB), (HD // 2, B), (1, HD // 2)]),
                    view(keys, at, [(B * KW, LB), (KW, B), (1, HD // 2)]),
                    view(keys, at + HD // 2, [(B * KW, LB), (KW, B), (1, HD // 2)]), ALU.mult)\
                    .then_inc(z_ready, 1)

            make_z(0)
            make_z(1)

            for h in range(H):
                pool.wait_ge(q_ready, h + 1)
                for b in range(LB):
                    pool.wait_ge(y_ready_b, h * LB + b + 1)
                    await_count(pool, att_ready_b, (h - 1) * LB + b + 1 if h else 0)
                    at_y = (h % 2 * LB + b) * (D_FULL + 1) * B * YW
                    at_q = (h % 2 * LB + b) * B * QW
                    nc.gpsimd.tensor_tensor(
                        view(prods, b * ROWS * HD + D_FULL + 1, [(1, D_FULL - 1), (HD * HD, B), (HD, HD)]),
                        view(y, at_y + B * YW + YPAD - 1, [(B * YW - 1, D_FULL - 1), (YW, B), (1, HD)]),
                        view(queries, at_q + YPAD - 1, [(-1, D_FULL - 1), (QW, B), (1, HD)]),
                        ALU.mult).then_inc(far_done_b, 1)
                if h + 2 < H:
                    make_z(h + 2)
                if h == 0:
                    nc.gpsimd.memset(empty[:], 0.0).then_inc(empty_cleared, 1)
                    pool.wait_ge(empty_cleared, 1)
                    nc.gpsimd.iota(empty[:, :, L:L + 1].bitcast(I32), [[P, SPARE], [0, 1]], base=SLOTS,
                                   channel_multiplier=1).then_inc(empty_ready, 1)
                    nc.gpsimd.memset(before[:], 1.0).then_inc(masks_set, 1)
                    pool.wait_ge(masks_set, 2)
                    nc.gpsimd.affine_select(out=before[:], in_=before[:], compare_op=ALU.is_gt, fill=0.0,
                                            base=0, pattern=[[1, P]], channel_multiplier=-1)
                    nc.gpsimd.memset(rows[:, :, :, L:RW], 0.0)
                    nc.gpsimd.memset(ones[:], 1.0)
                    nc.gpsimd.memset(ones_row[:], 1.0)
                    nc.gpsimd.iota(row_id[:], [[P, H], [H * P, TOPK]], base=0, channel_multiplier=1)
                    nc.gpsimd.iota(down[:], [[-1, E]], base=E, channel_multiplier=0,
                                   allow_small_or_imprecise_dtypes=True)
                    nc.gpsimd.iota(fills[:], [[P, H]], base=0, channel_multiplier=0,
                                   allow_small_or_imprecise_dtypes=True)
                    nc.gpsimd.iota(tile_id[:], [[1, TILES]], base=0, channel_multiplier=0,
                                   allow_small_or_imprecise_dtypes=True).then_inc(consts_ready, 1)

            pool.wait_ge(rows_emptied, 16)
            pool.wait_ge(slots_ready, 1)
            for n in range(H):
                pool.wait_ge(rows_ready, n + 1)
                for k in range(TOPK):
                    nc.gpsimd.indirect_dma_start(
                        routed_in, bass.IndirectOffsetOnAxis(ap=slot_of[:, k, n:n + 1].bitcast(U32), axis=0),
                        rows[:, n % ROUND, k], None).then_inc(scattered[n % ROUND], 16)

            for t in range(TILES):
                if t >= SPARE:
                    u = t - SPARE
                    pool.wait_ge(r_stored[u % RR], 16 * (u // RR + 1))
                pool.wait_ge(ro_ready, t + 1)
                nc.gpsimd.indirect_dma_start(
                    routed_out, bass.IndirectOffsetOnAxis(ap=r_in[:, t % RR, L:L + 1].bitcast(U32), axis=0),
                    r_out[:, t % RR], None).then_inc(r_stored[t % RR], 16)

        @block.scalar
        def _(act):
            act.dma_start(filt[:, P - 1:P - 1 + L], taps).then_inc(taps_loaded, 16)
            act.dma_start(skip_sb[:, :], skip).then_inc(taps_loaded, 16)
            act.dma_start(gates[:, 0:1], g_xattn.partition_broadcast(P)).then_inc(gates_loaded, 16)
            act.dma_start(gates[:, 1:2], g_ffn.partition_broadcast(P)).then_inc(gates_loaded, 16)
            act.wait_ge(gates_loaded, 32)
            nc.scalar.activation(tanh_g[:], gates[:], ACT.Tanh).then_inc(tanh_ready, 1)
            act.wait_ge(eps_ready, 1)

            def root_var1(c):
                act.wait_ge(var1_ready, c + 1)
                now = slice(CHUNK * c, CHUNK * (c + 1))
                nc.scalar.activation(std1[:, now], var1[:, now], ACT.Sqrt, bias=eps[:, 0:1]).then_inc(std1_ready, 1)

            def norm_x(h):
                act.wait_ge(shift1_ready, h // CHUNK + 1)
                await_count(act, q_done, h - 1)
                nc.scalar.activation(xq[:, h % 2], x_all[:, h], ACT.Identity, bias=shift1[:, h:h + 1],
                                     scale=rstd1[:, h:h + 1]).then_inc(xq_ready, 1)

            def load_queries(h):
                act.wait_ge(q_done, h + 1)
                await_count(act, near_done_b, (h - 1) * LB)
                await_count(act, far_done_b, (h - 1) * LB)
                src = q_ps.rearrange("p (r i) -> p r i", i=HD)
                dst = queries[:, h % 2].rearrange("p l (b i) -> p (l b) i", i=QW)
                nc.scalar.activation(dst[:, :, YPAD:YPAD + HD], src, ACT.Copy)
                nc.scalar.activation(dst[:, :, 0:YPAD], src[:, :, HD - YPAD:HD], ACT.Copy)
                nc.scalar.activation(dst[:, :, YPAD + HD:YPAD + HD + D_FULL], src[:, :, 0:D_FULL], ACT.Copy)\
                    .then_inc(q_ready, 1)

            def load_y(h, b):
                act.wait_ge(y_done_b, h * LB + b + 1)
                if h >= 2:
                    act.wait_ge(near_done_b, (h - 2) * LB + b + 1)
                    act.wait_ge(far_done_b, (h - 2) * LB + b + 1)
                src = y_ps[b][:, :].rearrange("p (r i) -> p r i", i=HD)
                dst = y[:, h % 2, b].rearrange("p (r i) -> p r i", i=YW)
                nc.scalar.activation(dst[:, 0:D_FULL * B, YPAD:YW], src, ACT.Copy)
                nc.scalar.activation(dst[:, B:D_FULL * B, 0:YPAD], src[:, B:D_FULL * B, HD - YPAD:HD], ACT.Copy)
                src4 = y4_ps[b]
                nc.scalar.activation(
                    view(y, ((h % 2 * LB + b) * (D_FULL + 1) + D_FULL) * B * YW + YPAD,
                         [(YW, B), (HD // 2, 2), (1, HD // 2)]),
                    bass.AP(src4.tensor, src4.offset, [list(src4.ap[0]), [HD // 2, B], [0, 2], [1, HD // 2]]),
                    ACT.Copy).then_inc(y_ready_b, 1)

            def deviation(h):
                act.wait_ge(mv_ready, h + 1)
                await_count(act, rstd_ready, h - 1)
                nc.scalar.activation(std2[:, h % 2:h % 2 + 1], mv2[:, h % 2, 1:2], ACT.Sqrt,
                                     bias=eps[:, 0:1]).then_inc(std_ready, 1)

            def norm_x1(h):
                act.wait_ge(shift_ready, h + 1)
                nc.scalar.activation(xn_all[:, h], x_all[:, h], ACT.Identity, bias=shift2[:, h % 2:h % 2 + 1],
                                     scale=rstd2[:, h % 2:h % 2 + 1]).then_inc(xn_ready, 1)

            def load_xnT(h):
                act.wait_ge(xnT_done, h + 1)
                nc.scalar.activation(xnT_all[:, :, h * P:(h + 1) * P], xnT_ps.rearrange("p (c t) -> p c t", c=LB),
                                     ACT.Copy).then_inc(xnT_ready, 1)

            def load_logits(h):
                act.wait_ge(gate_done, h + 1)
                nc.scalar.activation(logits[:, h], gate_ps, ACT.Copy).then_inc(logits_ready, 1)

            root_var1(0)
            norm_x(0)
            norm_x(1)
            load_queries(0)
            for h in range(H + 3):
                if h < H:
                    load_y(h, 0)
                if 2 <= h < H + 2:
                    norm_x1(h - 2)
                if h < H:
                    load_y(h, 1)
                if h + 1 < H:
                    load_queries(h + 1)
                if h % CHUNK == 1 and h // CHUNK + 1 < NCHUNK:
                    root_var1(h // CHUNK + 1)
                if 1 <= h < H + 1:
                    deviation(h - 1)
                if h >= 3:
                    load_logits(h - 3)
                if 2 <= h < H + 2:
                    load_xnT(h - 2)
                if h + 2 < H:
                    norm_x(h + 2)

            act.wait_ge(logits_ready, H)
            nc.scalar.activation(probs[:], logits[:], ACT.Sigmoid).then_inc(probs_ready, 1)
            for c in range(NCHUNK):
                act.wait_ge(up_done, c + 1)
                await_count(act, sh_ready, c - 1)
                nc.scalar.activation(shared_act[:, c % 2], up_ps[c % 2][0][:, :], ACT.Silu)\
                    .then_inc(sact_ready, 1)

            for t in range(TILES + 3):
                if t < TILES:
                    act.wait_ge(rT_done, t + 1)
                    await_count(act, ru_done, t - 1)
                    nc.scalar.activation(r_inT[:, t % 2], rT_ps[t % 2].rearrange("p (c t) -> p c t", c=LB),
                                         ACT.Copy).then_inc(rT_ready, 1)
                u = t - 1
                if 0 <= u < TILES:
                    act.wait_ge(ru_done, u + 1)
                    await_count(act, rh_ready, u - 1)
                    nc.scalar.activation(r_act[:, u % 2], ru_ps[u % 2][:, 0:HID], ACT.Silu).then_inc(ract_ready, 1)
                v = t - 3
                if v >= 0:
                    act.wait_ge(ro_done, v + 1)
                    if v >= RR:
                        act.wait_ge(r_stored[v % RR], 16 * (v // RR))
                    nc.scalar.activation(r_out[:, v % RR], ro_ps[v % 2], ACT.Copy).then_inc(ro_ready, 1)

            for h in range(H):
                act.wait_ge(final_ready, h + 1)
                act.dma_start(out[:, h], final[:, h % ROUND]).then_inc(out_stored[h % ROUND], 16)

        @block.vector
        def _(dve):
            nc.vector.memset(filt[:, 0:P - 1], 0.0)
            nc.vector.memset(filt[:, P - 1 + L:KPAD], 0.0).then_inc(filt_zeroed, 1)
            nc.vector.memset(eps[:], EPS).then_inc(eps_ready, 1)
            dve.wait_ge(taps_loaded, 32)
            dve.wait_ge(filt_zeroed, 1)
            nc.vector.tensor_tensor(filt[:, P - 1:P], filt[:, P - 1:P], skip_sb[:, :], ALU.add)\
                .then_inc(filt_ready, 1)

            links = [0]

            def link1(ins):
                links[0] += 1
                ins.then_inc(norm1, 1)
                dve.wait_ge(norm1, links[0])

            def variances(c):
                now = slice(CHUNK * c, CHUNK * (c + 1))
                dve.wait_ge(x_loaded[c], 16)
                for h in range(CHUNK * c, CHUNK * (c + 1)):
                    last = nc.vector.bn_stats(st1[:, h, :], x_all[:, h])
                link1(last)
                nc.vector.tensor_tensor(sum1[:, now], st1[:, now, 1], st1[:, now, 4], ALU.add)
                nc.vector.tensor_tensor(half1[:, now], st1[:, now, 1], st1[:, now, 4], ALU.subtract)
                link1(nc.vector.tensor_tensor(var1[:, now], st1[:, now, 2], st1[:, now, 5], ALU.add))
                link1(nc.vector.scalar_tensor_tensor(half1[:, now], half1[:, now], 0.25 * L, half1[:, now],
                                                     ALU.mult, ALU.mult))
                link1(nc.vector.tensor_tensor(var1[:, now], var1[:, now], half1[:, now], ALU.add))
                nc.vector.tensor_scalar(var1[:, now], var1[:, now], 1.0 / L, None, ALU.mult).then_inc(var1_ready, 1)

            def shifts(c):
                now = slice(CHUNK * c, CHUNK * (c + 1))
                dve.wait_ge(std1_ready, c + 1)
                link1(nc.vector.reciprocal(rstd1[:, now], std1[:, now]))
                nc.vector.scalar_tensor_tensor(shift1[:, now], sum1[:, now], -0.5, rstd1[:, now],
                                               ALU.mult, ALU.mult).then_inc(shift1_ready, 1)

            def near(h, b):
                dve.wait_ge(y_ready_b, h * LB + b + 1)
                if h:
                    dve.wait_ge(att_ready_b, (h - 1) * LB + b + 1)
                at_y = (h % 2 * LB + b) * (D_FULL + 1) * B * YW
                at_q = (h % 2 * LB + b) * B * QW
                nc.vector.tensor_tensor(
                    view(prods, b * ROWS * HD, [(1, D_FULL + 1), (HD * HD, B), (HD, HD)]),
                    view(y, at_y + YPAD, [(B * YW, D_FULL + 1), (YW, B), (1, HD)]),
                    view(queries, at_q + YPAD, [(1, D_FULL + 1), (QW, B), (1, HD)]),
                    ALU.mult).then_inc(near_done_b, 1)

            def attend(h, b):
                dve.wait_ge(near_done_b, h * LB + b + 1)
                dve.wait_ge(far_done_b, h * LB + b + 1)
                await_count(dve, att_done, h - 1)
                nc.vector.tensor_reduce(att[:, h % 2, b], prods[:, b].rearrange("p (r t) -> p r t", t=HD),
                                        AX_X, ALU.add).then_inc(att_ready_b, 1)

            def add_attention(h):
                dve.wait_ge(att_done, h + 1)
                nc.vector.scalar_tensor_tensor(x_all[:, h], att_ps, tanh_g[:, 0:1], x_all[:, h], ALU.mult, ALU.add)\
                    .then_inc(x1_ready, 1)
                dve.wait_ge(x1_ready, h + 1)
                nc.vector.bn_stats(st2[:, h % 2], x_all[:, h]).then_inc(stats_ready, 1)
                dve.wait_ge(stats_ready, h + 1)
                await_count(dve, std_ready, h - 1)
                await_count(dve, shift_ready, h - 1)
                nc.vector.bn_aggr(mv2[:, h % 2], st2[:, h % 2]).then_inc(mv_ready, 1)

            def shift_x1(h):
                dve.wait_ge(std_ready, h + 1)
                await_count(dve, xn_ready, h - 1)
                nc.vector.reciprocal(rstd2[:, h % 2:h % 2 + 1], std2[:, h % 2:h % 2 + 1]).then_inc(rstd_ready, 1)
                dve.wait_ge(rstd_ready, h + 1)
                nc.vector.scalar_tensor_tensor(shift2[:, h % 2:h % 2 + 1], mv2[:, h % 2, 0:1], -1.0,
                                               rstd2[:, h % 2:h % 2 + 1], ALU.mult, ALU.mult)\
                    .then_inc(shift_ready, 1)

            variances(0)
            shifts(0)
            dve.wait_ge(tanh_ready, 1)
            for h in range(H + 1):
                if h < H:
                    dve.wait_ge(q_ready, h + 1)
                    near(h, 0)
                if h % CHUNK == 0 and h // CHUNK + 1 < NCHUNK:
                    variances(h // CHUNK + 1)
                if h < H:
                    attend(h, 0)
                if h >= 1:
                    add_attention(h - 1)
                if h < H:
                    near(h, 1)
                if h % CHUNK == 1 and h // CHUNK + 1 < NCHUNK:
                    shifts(h // CHUNK + 1)
                if h >= 1:
                    shift_x1(h - 1)
                if h < H:
                    attend(h, 1)

            steps = [0]

            def link(ins):
                steps[0] += 1
                ins.then_inc(route, 1)
                dve.wait_ge(route, steps[0])

            dve.wait_ge(consts_ready, 1)
            dve.wait_ge(probs_ready, 1)
            down_b = view(down, 0, [(0, H), (1, E)])

            def best(of, k):
                top = score[:, :, k:k + 1].broadcast_to([P, H, E])
                link(nc.vector.tensor_reduce(score[:, :, k], of[:], AX_X, ALU.max))
                link(nc.vector.tensor_tensor(is_max[:], of[:], top, ALU.is_equal))
                link(nc.vector.tensor_tensor(rank[:], is_max[:], down_b, ALU.mult))
                link(nc.vector.tensor_reduce(top_rank[:, :, k], rank[:], AX_X, ALU.max))
                link(nc.vector.tensor_tensor(chosen[:, k], down_b,
                                             top_rank[:, :, k:k + 1].broadcast_to([P, H, E]), ALU.is_equal))

            best(probs, 0)
            link(nc.vector.scalar_tensor_tensor(rest[:], chosen[:, 0], -2.0, probs[:], ALU.mult, ALU.add))
            best(rest, 1)
            nc.vector.tensor_tensor(mask[:].rearrange("p (h e) -> p h e", h=H), chosen[:, 0], chosen[:, 1],
                                    ALU.add).then_inc(mask_ready, 1)

            def make_rows(n):
                await_count(dve, scattered[n % ROUND], 16 * TOPK * (n // ROUND))
                for k in range(TOPK):
                    nc.vector.tensor_scalar(rows[:, n % ROUND, k, 0:L], xn_all[:, n], score[:, n, k:k + 1], None,
                                            ALU.mult)
                nc.vector.tensor_copy(rows[:, n % ROUND, :, L:L + 1].bitcast(I32), row_id[:, n, :].unsqueeze(2))\
                    .then_inc(rows_ready, 1)

            make_rows(0)
            make_rows(1)

            dve.wait_ge(place_done, 1)
            link(nc.vector.tensor_reduce(count[:], total_ps.rearrange("p (h e) -> p e h", h=H), AX_X, ALU.add))
            link(nc.vector.tensor_tensor(over[:], view(count, 0, [(1, E), (0, H)]), view(fills, 0, [(0, E), (1, H)]),
                                         ALU.is_gt))
            link(nc.vector.tensor_reduce(tiles[:], over[:], AX_X, ALU.add))
            link(nc.vector.tensor_tensor_scan(tiles_to[:], ones_row[:], tiles[:], 0.0, ALU.mult, ALU.add))
            link(nc.vector.tensor_tensor(tiles_before[:], tiles_to[:], tiles[:], ALU.subtract))
            link(nc.vector.scalar_tensor_tensor(place[:], view(tiles_before, 0, [(0, H), (1, E)]), float(P),
                                                place_ps.rearrange("p (h e) -> p h e", h=H), ALU.mult, ALU.add))
            for k in range(TOPK):
                last = nc.vector.tensor_tensor(picked[:, k], chosen[:, k], place[:], ALU.mult)
            link(last)
            link(nc.vector.tensor_reduce(slot_f[:], picked[:], AX_X, ALU.add))
            nc.vector.tensor_copy(slot_of[:], slot_f[:]).then_inc(slots_ready, 1)
            link(nc.vector.tensor_tensor(
                ended[:], bass.AP(tiles_to[:].tensor, tiles_to[:].offset, [list(tiles_to[0:1].ap[0]), [0, TILES], [1, E]]),
                bass.AP(tile_id[:].tensor, tile_id[:].offset, [list(tile_id[0:1].ap[0]), [1, TILES], [0, E]]),
                ALU.is_le))
            link(nc.vector.tensor_reduce(tile_expert_f[:], ended[:], AX_X, ALU.add))
            nc.vector.tensor_scalar(tile_expert[:], tile_expert_f[:], float(E - 1), None, ALU.min)\
                .then_inc(table_ready, 1)

            for c in range(NCHUNK):
                dve.wait_ge(sact_ready, c + 1)
                await_count(dve, sout_done, CHUNK * (c - 1))
                nc.vector.tensor_tensor(shared_h[:, c % 2], shared_act[:, c % 2], up_ps[c % 2][1][:, :], ALU.mult)\
                    .then_inc(sh_ready, 1)
                for n in range(CHUNK * c, CHUNK * c + CHUNK):
                    if n >= 2:
                        make_rows(n)
                for n in range(CHUNK * c, CHUNK * c + CHUNK):
                    dve.wait_ge(sout_done, n + 1)
                    dve.wait_ge(rows_ready, n + 1)
                    nc.vector.scalar_tensor_tensor(xn_all[:, n], sh_ps[n % CHUNK], tanh_g[:, 1:2], x_all[:, n],
                                                   ALU.mult, ALU.add).then_inc(base_ready, 1)

            for t in range(TILES + 2):
                w = t - 2
                if w >= 0:
                    dve.wait_ge(rhT_done, w + 1)
                    await_count(dve, ro_done, w - 1)
                    nc.vector.tensor_copy(r_hT[:, w % 2], rh_ps[w % 2]).then_inc(rhT_ready, 1)
                u = t - 1
                if 0 <= u < TILES:
                    dve.wait_ge(ract_ready, u + 1)
                    await_count(dve, rhT_done, u - 1)
                    nc.vector.tensor_tensor(r_h[:, u % 2], r_act[:, u % 2], ru_ps[u % 2][:, HID:2 * HID],
                                            ALU.mult).then_inc(rh_ready, 1)

            dve.wait_ge(base_ready, H)
            for n in range(H):
                dve.wait_ge(results_loaded[n % ROUND], 16 * (n // ROUND + 1))
                await_count(dve, final_ready, n - 1)
                nc.vector.tensor_tensor(both[:, n % 2], results[:, n % ROUND, 0], results[:, n % ROUND, 1], ALU.add)\
                    .then_inc(both_ready, 1)
                dve.wait_ge(both_ready, n + 1)
                await_count(dve, out_stored[n % ROUND], 16 * (n // ROUND))
                nc.vector.scalar_tensor_tensor(final[:, n % ROUND], both[:, n % 2], tanh_g[:, 1:2], xn_all[:, n],
                                               ALU.mult, ALU.add).then_inc(final_ready, 1)

        @block.tensor
        def _(pe):
            def transpose_q(h):
                pe.wait_ge(xq_ready, h + 1)
                await_count(pe, q_ready, h)
                for b in range(LB):
                    last = nc.tensor.transpose(q_ps[:, b * P:(b + 1) * P], xq[:, h % 2, b * P:(b + 1) * P], ident[:])
                last.then_inc(q_done, 1)

            def convolve(h):
                pe.wait_ge(toep_loaded[h % KR], 16 * (h // KR + 1))
                pe.wait_ge(z_ready, h + 1)
                same, previous = toep[:, h % KR, 0:P], toep[:, h % KR, P:2 * P]
                for b, terms in enumerate([[(same, 0)], [(previous, 0), (same, 1)]]):
                    if h:
                        pe.wait_ge(y_ready_b, (h - 1) * LB + b + 1)
                    for n, (w, m) in enumerate(terms):
                        flags = dict(start=(n == 0), stop=(n == len(terms) - 1))
                        nc.tensor.matmul(y_ps[b][:, :], w, z[:, h % 2, m, 0:PAIRS], **flags)
                        last = nc.tensor.matmul(y4_ps[b], w, z[:, h % 2, m, PAIRS:ZW], **flags)
                    last.then_inc(y_done_b, 1)

            def transpose_att(h):
                pe.wait_ge(att_ready_b, (h + 1) * LB)
                await_count(pe, x1_ready, h)
                for b in range(LB):
                    last = nc.tensor.transpose(att_ps[:, b * P:(b + 1) * P], att[:, h % 2, b], ident[:])
                last.then_inc(att_done, 1)

            def transpose_xn(h):
                pe.wait_ge(xn_ready, h + 1)
                await_count(pe, xnT_ready, h)
                for b in range(LB):
                    last = nc.tensor.transpose(xnT_ps[:, b * P:(b + 1) * P], xn_all[:, h, b * P:(b + 1) * P], ident[:])
                last.then_inc(xnT_done, 1)

            def gate(h):
                pe.wait_ge(xnT_ready, h + 1)
                await_count(pe, logits_ready, h)
                for b in range(LB):
                    last = nc.tensor.matmul(gate_ps, xnT_all[:, b, h * P:(h + 1) * P], gate_sb[:, b], start=(b == 0),
                                            stop=(b == LB - 1))
                last.then_inc(gate_done, 1)

            pe.wait_ge(ident_ready, 1)
            transpose_q(0)
            for h in range(H + 3):
                if h < H:
                    convolve(h)
                if h + 1 < H:
                    transpose_q(h + 1)
                if 1 <= h < H + 1:
                    transpose_att(h - 1)
                if h == 3:
                    pe.wait_ge(gatew_loaded, 16)
                if h >= 3:
                    gate(h - 3)
                if 2 <= h < H + 2:
                    transpose_xn(h - 2)

            pe.wait_ge(shared_loaded, 32)
            pe.wait_ge(xnT_ready, H)
            pe.wait_ge(y_ready_b, H * LB)

            def up(c):
                await_count(pe, sh_ready, c - 1)
                for j in range(2):
                    for b in range(LB):
                        last = nc.tensor.matmul(up_ps[c % 2][j][:, :], sw13_sb[:, b, j * HID:(j + 1) * HID],
                                                xnT_all[:, b, c * CHUNK * P:(c + 1) * CHUNK * P],
                                                start=(b == 0), stop=(b == LB - 1))
                last.then_inc(up_done, 1)

            def count_rows():
                pe.wait_ge(consts_ready, 1)
                pe.wait_ge(mask_ready, 1)
                nc.tensor.matmul(place_ps, before[:], mask[:], start=True, stop=False)
                for h in range(H - 1):
                    nc.tensor.matmul(place_ps[:, (h + 1) * E:H * E], ones[:],
                                     view(mask, h * E, [(0, H - 1 - h), (1, E)]),
                                     start=False, stop=(h == H - 2))
                nc.tensor.matmul(total_ps, ones[:], mask[:], start=True, stop=True).then_inc(place_done, 1)

            up(0)
            up(1)
            count_rows()
            pe.wait_ge(x1_ready, H)
            for c in range(NCHUNK):
                pe.wait_ge(sh_ready, c + 1)
                for t in range(CHUNK):
                    await_count(pe, base_ready, CHUNK * (c - 1) + t + 1)
                    nc.tensor.matmul(sh_ps[t], shared_h[:, c % 2, t * P:(t + 1) * P], sw2_sb[:], start=True,
                                     stop=True).then_inc(sout_done, 1)
                if c + 2 < NCHUNK:
                    up(c + 2)

            pe.wait_ge(experts_loaded, 32)
            pe.wait_ge(table_ready, 1)
            pe.wait_ge(base_ready, H)
            pe.wait_ge(sh_ready, NCHUNK)
            expert = {}
            for t in range(TILES + 3):
                if t < TILES:
                    expert[t] = pe.value_load(tile_expert[0:1, t:t + 1], min_val=0, max_val=E - 1)
                    pe.wait_ge(r_loaded[t % RR], 16 * (t // RR + 1))
                    await_count(pe, rT_ready, t - 1)
                    for b in range(LB):
                        last = nc.tensor.transpose(rT_ps[t % 2][:, b * P:(b + 1) * P],
                                                   r_in[:, t % RR, b * P:(b + 1) * P], ident[:])
                    last.then_inc(rT_done, 1)
                u = t - 1
                if 0 <= u < TILES:
                    pe.wait_ge(rT_ready, u + 1)
                    await_count(pe, rh_ready, u - 1)
                    for b in range(LB):
                        last = nc.tensor.matmul(ru_ps[u % 2], r_inT[:, u % 2, b],
                                                w13_sb[:, b, bass.ds(expert[u] * (2 * HID), 2 * HID)],
                                                start=(b == 0), stop=(b == LB - 1))
                    last.then_inc(ru_done, 1)
                v = t - 3
                if v >= 0:
                    pe.wait_ge(rhT_ready, v + 1)
                    await_count(pe, ro_ready, v - 1)
                    nc.tensor.matmul(ro_ps[v % 2], r_hT[:, v % 2], w2_sb[:, bass.ds(expert.pop(v) * L, L)],
                                     start=True, stop=True).then_inc(ro_done, 1)
                w = t - 2
                if 0 <= w < TILES:
                    pe.wait_ge(rh_ready, w + 1)
                    await_count(pe, rhT_ready, w - 1)
                    nc.tensor.transpose(rh_ps[w % 2], r_h[:, w % 2], ident[:]).then_inc(rhT_done, 1)


def kernel(x, ctx_2048, g_xattn, g_ffn, L0_xattn_ssm_kernel, L0_xattn_D, L0_ffn_gate_w, L0_ffn_w1, L0_ffn_w2,
           L0_ffn_w3, L0_ffn_sw1, L0_ffn_sw2, L0_ffn_sw3):
    import numpy as np
    import concourse.bacc as bacc
    from concourse.bass_utils import run_bass_kernel_spmd

    def kmajor(w):
        return w.T.reshape(LB, P, -1).transpose(1, 0, 2)

    xs = x.reshape(B, H, HD, L).transpose(0, 2, 1, 3).reshape(P, H, L)
    c = ctx_2048.reshape(B, H, HD, LB, P)[..., ::-1].transpose(1, 4, 3, 0, 2)
    c = np.concatenate([c, c[..., :D_FULL]], axis=-1).reshape(H, P, LB, B * KW)
    w13 = np.stack([np.concatenate([kmajor(L0_ffn_w1[e]), kmajor(L0_ffn_w3[e])], axis=-1) for e in range(E)], axis=2)
    arrays = {
        "x": xs,
        "ctx": c,
        "g_xattn": g_xattn,
        "g_ffn": g_ffn,
        "taps": L0_xattn_ssm_kernel,
        "skip": L0_xattn_D.reshape(H, 1),
        "gate_w": kmajor(L0_ffn_gate_w),
        "w13": w13.reshape(P, LB, E * 2 * HID),
        "w2": L0_ffn_w2.transpose(2, 0, 1).reshape(HID, E * L),
        "sw13": np.concatenate([kmajor(L0_ffn_sw1), kmajor(L0_ffn_sw3)], axis=-1),
        "sw2": L0_ffn_sw2.T,
    }
    arrays = {name: np.ascontiguousarray(a) for name, a in arrays.items()}
    nc = bacc.Bacc("TRN2", target_bir_lowering=False, num_devices=1)
    aps = [nc.dram_tensor(f"in_{name}", a.shape, mybir.dt.from_np(a.dtype), kind="ExternalInput").ap()
           for name, a in arrays.items()]
    out = nc.dram_tensor("out", [P, H, L], F32, kind="ExternalOutput").ap()
    flamingo_block(nc, *aps, out)
    done = run_bass_kernel_spmd(nc, [{f"in_{name}": a for name, a in arrays.items()}], core_ids=[0])
    got = done.results[0]["out"]
    return np.ascontiguousarray(got.reshape(B, HD, H, L).transpose(0, 2, 1, 3).reshape(B, H * HD, L))
```

```python
from contextlib import ExitStack

import concourse.bass as bass
from concourse import mybir

ALU = mybir.AluOpType
ACT = mybir.ActivationFunctionType
F32 = mybir.dt.float32
BF16 = mybir.dt.bfloat16
I32 = mybir.dt.int32
U32 = mybir.dt.uint32
AX_X = mybir.AxisListType.X

P = 128
H = 16
B = 16
HD = 8
L = 256
LB = L // P
E = 8
TOPK = 2
HID = 128
EPS = 1e-5

D_FULL = HD // 2
PAIRS = D_FULL * B * HD
PAIRS4 = B * HD // 2
ZW = PAIRS + PAIRS4
KW = HD + D_FULL
YW = HD + D_FULL - 1
YPAD = D_FULL - 1
QW = 16
ROWS = B * HD

NORMED = (2, 4, 5, 5)
NORM_END = [sum(NORMED[:c + 1]) for c in range(len(NORMED))]
CHUNK = 4
NCHUNK = H // CHUNK
SLOTS = H * ROWS * TOPK
TILES = SLOTS // P + E - 1
KPAD = 384
ROUND = 6
RW = L + 4
CAP = H * ROWS + P
SETS = 2 * E
GROUPS = (8, 8)
GROUP_END = [sum(GROUPS[:g + 1]) for g in range(len(GROUPS))]
GROUP_MAX = max(GROUPS)
EARLY = H - GROUPS[-1]
SEND_LAG = 6
KR = 4
PARTS = (4, 1)
RO = 4
RR = 12


def await_count(eng, sem, n):
    if n > 0:
        eng.wait_ge(sem, n)


def on_first(tensor, dims):
    whole = tensor[0:1]
    return bass.AP(whole.tensor, whole.offset, [list(whole.ap[0])] + [list(d) for d in dims])


def group_of(h):
    return next(g for g, end in enumerate(GROUP_END) if h < end)


def sent_at(step):
    steps, at = [], 0
    for n in range(EARLY):
        ready = GROUP_END[group_of(n)] - 1 + SEND_LAG
        at = max(at + 1 if at < H or steps.count(at) == 2 else at, ready)
        steps.append(at)
    return [n for n in range(EARLY) if steps[n] == step]


def late_rows(c):
    late = list(range(EARLY + ROUND, H))
    return late[:len(late) // 2] if c == 2 else late[len(late) // 2:]


def measured_at(n):
    return 0 if n < NORM_END[1] else max(n - 7, 1)


def starting(steps_ahead, step):
    return [c + 1 for c, first in enumerate(NORM_END[:-1]) if max(first - steps_ahead, 0) == step]


def opposite_on_pool(h):
    return not sent_at(h - 3)


def view(tensor, offset, dims):
    whole = tensor[:]
    return bass.AP(whole.tensor, offset + whole.offset, [list(whole.ap[0])] + [list(d) for d in dims])


def flamingo_block(nc, x, ctx, both_gates, skip_and_taps, gate_w, w13, w2, sw13, sw2, out):
    filt_dram = nc.dram_tensor("filt_dram", [H, KPAD], F32, kind="Internal").ap()
    routed_in = nc.dram_tensor("routed_in", [E * CAP + E * P, RW], F32, kind="Internal").ap()

    with ExitStack() as stack:
        def sb(name, shape, dt=F32):
            return stack.enter_context(nc.sbuf_tensor(name, shape, dt))

        def sem(name):
            return stack.enter_context(nc.semaphore(name))

        ident = sb("ident", [P, P])
        before = sb("before", [P, P], BF16)
        ones = sb("ones", [P, P], BF16)
        ones_row = sb("ones_row", [P, E])
        down = sb("down", [P, E])
        fills = sb("fills", [P, E, H])
        tile_id = sb("tile_id", [P, TILES])
        tile_at = sb("tile_at", [P, TILES])
        tile_adds = sb("tile_adds", [P, -(-TILES // RO), RO])
        row_id = sb("row_id", [P, H, 1], I32)
        empty = sb("empty", [P, SETS, RW])
        eps = sb("eps", [P, 1])
        spare_act = sb("spare_act", [P, 3])
        gates = sb("gates", [P, 2])
        tanh_g = sb("tanh_g", [P, 2])
        filt = sb("filt", [H, KPAD])
        gate_sb = sb("gate_sb", [P, LB, E])
        w13_sb = sb("w13_sb", [P, LB, E * 2 * HID])
        w2_sb = sb("w2_sb", [P, E * L])
        sw13_sb = sb("sw13_sb", [P, LB, 2 * HID])
        sw2_sb = sb("sw2_sb", [P, L])
        x_all = sb("x_all", [P, H, L])
        xn_all = sb("xn_all", [P, H, L])
        xnT_all = sb("xnT_all", [P, LB, H * P])
        st1 = sb("st1", [P, H, 6])
        mv1 = sb("mv1", [P, H, 2])
        std1 = sb("std1", [P, H])
        rstd1 = sb("rstd1", [P, H])
        shift1 = sb("shift1", [P, H])
        keys = sb("keys", [P, KR, LB, B * KW])
        toep = sb("toep", [P, KR, L])
        z = sb("z", [P, 2, LB, ZW])
        xq = sb("xq", [P, 2, L])
        queries = sb("queries", [P, 2, LB, B * QW])
        y = sb("y", [P, 2, LB, (D_FULL + 1) * B * YW])
        prods = sb("prods", [P, LB, ROWS * HD])
        att = sb("att", [P, 2, LB, HD // 2, ROWS])
        st2 = sb("st2", [P, 2, 6])
        mv2 = sb("mv2", [P, 2, 2])
        std2 = sb("std2", [P, 2])
        rstd2 = sb("rstd2", [P, 2])
        shift2 = sb("shift2", [P, 2])
        logits = sb("logits", [P, H, E])
        probs = sb("probs", [P, H, E])
        score = sb("score", [P, H, TOPK])
        is_max = sb("is_max", [P, H, E])
        rank = sb("rank", [P, H, E])
        top_rank = sb("top_rank", [P, H, TOPK])
        chosen = sb("chosen", [P, TOPK, H, E])
        rest = sb("rest", [P, H, E])
        mask = sb("mask", [P, len(GROUPS), (GROUP_MAX + 1) * E], BF16)
        place = sb("place", [P, len(GROUPS), GROUP_MAX + 1, E])
        next_row = sb("next_row", [P, E])
        at_row = sb("at_row", [P, GROUP_MAX, E])
        picked = sb("picked", [P, TOPK, GROUP_MAX, E])
        slot_f = sb("slot_f", [P, TOPK, H])
        slot_of = sb("slot_of", [P, TOPK, H], I32)
        pad_row = sb("pad_row", [1, E], I32)
        over = sb("over", [1, E, H])
        tiles = sb("tiles", [1, E])
        tiles_to = sb("tiles_to", [1, E])
        skipped = sb("skipped", [1, E])
        ended = sb("ended", [1, TILES, E])
        jumps = sb("jumps", [1, TILES, E])
        jump = sb("jump", [1, TILES])
        tile_row_f = sb("tile_row_f", [1, TILES])
        tile_row = sb("tile_row", [1, TILES], I32)
        tile_expert_f = sb("tile_expert_f", [1, TILES])
        tile_expert = sb("tile_expert", [1, TILES], I32)
        waited = sb("waited", [1, TILES])
        new_expert = sb("new_expert", [1, TILES])
        adds_f = sb("adds_f", [1, TILES])
        adds = sb("adds", [1, 2, TILES], I32)
        rows = sb("rows", [P, ROUND, TOPK, RW])
        shared_act = sb("shared_act", [P, 2, CHUNK * P])
        shared_h = sb("shared_h", [P, 2, CHUNK * P])
        r_in = sb("r_in", [P, RR, RW])
        r_inT = sb("r_inT", [P, 2, LB, P])
        r_act = sb("r_act", [P, 2, HID])
        r_h = sb("r_h", [P, 2, HID])
        r_hT = sb("r_hT", [P, 2, P])
        r_out = sb("r_out", [P, RO, L])

        banks = [stack.enter_context(nc.psum_tensor(f"bank{n}", [P, 512], F32)) for n in range(8)]
        y_ps = [banks[0], banks[1]]
        y4_ps = [banks[2][:, 0:PAIRS4], banks[3][:, 0:PAIRS4]]
        q_ps = banks[4][:, 0:L]
        att_ps = banks[5][:, 0:L]
        xnT_ps = banks[6][:, 0:L]
        gate_ps = banks[7][:, 0:E]
        place_ps = banks[7][:, P:P + (GROUP_MAX + 1) * E]
        up_ps = [[banks[0], banks[1]], [banks[2], banks[3]]]
        sh_ps = [banks[4 + t][:, 0:L] for t in range(CHUNK)]
        rT_ps = [banks[0 + s][:, 0:256] for s in range(2)]
        ru_ps = [banks[2 + s][:, 0:256] for s in range(2)]
        rh_ps = [banks[4 + s][:, 0:P] for s in range(2)]
        ro_ps = [banks[6 + s][:, 0:256] for s in range(2)]

        x_loaded = [sem(f"x_loaded{c}") for c in range(len(NORMED))]
        taps_loaded = sem("taps_loaded")
        gates_loaded = sem("gates_loaded")
        gatew_loaded = sem("gatew_loaded")
        shared_loaded = sem("shared_loaded")
        experts_loaded = sem("experts_loaded")
        filt_zeroed = sem("filt_zeroed")
        skip_added = sem("skip_added")
        filt_ready = sem("filt_ready")
        filt_stored = sem("filt_stored")
        keys_loaded = [sem(f"keys_loaded{s}") for s in range(KR)]
        toep_loaded = [sem(f"toep_loaded{s}") for s in range(KR)]
        empty_cleared = sem("empty_cleared")
        empty_ready = sem("empty_ready")
        rows_emptied = sem("rows_emptied")
        masks_set = sem("masks_set")
        ident_ready = sem("ident_ready")
        consts_ready = sem("consts_ready")
        eps_ready = sem("eps_ready")
        tanh_ready = sem("tanh_ready")
        stats1_ready = sem("stats1_ready")
        rstd1_ready = sem("rstd1_ready")
        var1_ready = sem("var1_ready")
        std1_ready = sem("std1_ready")
        shift1_ready = sem("shift1_ready")
        z_ready = sem("z_ready")
        squares_ready = sem("squares_ready")
        opposite_ready = sem("opposite_ready")
        y_done_b = sem("y_done_b")
        y_ready_b = sem("y_ready_b")
        near_done_b = sem("near_done_b")
        far_done_b = sem("far_done_b")
        att_ready_b = sem("att_ready_b")
        xq_ready = sem("xq_ready")
        q_done = sem("q_done")
        q_ready = sem("q_ready")
        att_done = sem("att_done")
        x1_ready = sem("x1_ready")
        stats_ready = sem("stats_ready")
        mv_ready = sem("mv_ready")
        std_ready = sem("std_ready")
        rstd_ready = sem("rstd_ready")
        shift_ready = sem("shift_ready")
        xn_ready = sem("xn_ready")
        xnT_done = sem("xnT_done")
        xnT_ready = sem("xnT_ready")
        gate_done = sem("gate_done")
        logits_ready = sem("logits_ready")
        probs_ready = sem("probs_ready")
        route = sem("route")
        mask_ready = sem("mask_ready")
        place_done = sem("place_done")
        place_ready = sem("place_ready")
        ids_ready = sem("ids_ready")
        pads_ready = sem("pads_ready")
        pads_stored = sem("pads_stored")
        tile_rows_ready = sem("tile_rows_ready")
        slots_ready = sem("slots_ready")
        table_ready = sem("table_ready")
        up_done = sem("up_done")
        sact_ready = sem("sact_ready")
        sh_ready = sem("sh_ready")
        sout_done = sem("sout_done")
        base_ready = sem("base_ready")
        rows_ready = sem("rows_ready")
        scattered = [sem(f"scattered{s}") for s in range(ROUND)]
        r_loaded = [sem(f"r_loaded{s}") for s in range(RR)]
        rT_done = sem("rT_done")
        rT_ready = sem("rT_ready")
        ru_done = sem("ru_done")
        ract_ready = sem("ract_ready")
        rh_ready = sem("rh_ready")
        rhT_done = sem("rhT_done")
        rhT_ready = sem("rhT_ready")
        ro_done = sem("ro_done")
        ro_ready = sem("ro_ready")
        adds_ready = sem("adds_ready")
        bases_stored = sem("bases_stored")
        added = [sem(f"added{s}") for s in range(RO)]

        block = stack.enter_context(nc.Block())

        @block.sync
        def _(sp):
            def load_keys(h):
                await_count(sp, z_ready, h - KR + 1)
                await_count(sp, squares_ready, h - KR + 1)
                await_count(sp, opposite_ready, sum(not opposite_on_pool(n) for n in range(h - KR + 1)))
                sp.dma_start(keys[:, h % KR], ctx[h]).then_inc(keys_loaded[h % KR], 16)

            def load_toep(h):
                await_count(sp, y_done_b, (h - KR + 1) * LB)
                src = bass.AP(filt_dram.tensor, h * KPAD, [[1, P], [1, L]])
                sp.dma_start(toep[:, h % KR], src).then_inc(toep_loaded[h % KR], 16)

            def load_x(c):
                heads = slice(NORM_END[c] - NORMED[c], NORM_END[c])
                sp.dma_start(x_all[:, heads], x[:, heads]).then_inc(x_loaded[c], 16)

            load_keys(0)
            load_x(0)
            load_keys(1)
            sp.wait_ge(filt_ready, 1)
            sp.dma_start(filt_dram, filt[:, :]).then_inc(filt_stored, 16)
            sp.wait_ge(filt_stored, 16)
            load_toep(0)
            load_toep(1)
            load_x(1)
            load_keys(2)
            load_toep(2)
            load_x(2)
            load_keys(3)
            load_toep(3)
            load_x(3)
            sp.dma_start(gate_sb[:], gate_w).then_inc(gatew_loaded, 16)
            for h in range(KR, H):
                load_keys(h)
                load_toep(h)
                if h == KR + 6:
                    sp.wait_ge(empty_ready, 1)
                    sp.dma_start(routed_in[E * CAP:].rearrange("(n p) c -> p n c", p=P), empty[:, E:SETS])\
                        .then_inc(rows_emptied, 16)
                if h == KR + 2:
                    sp.dma_start(sw13_sb[:], sw13).then_inc(shared_loaded, 16)
                    sp.dma_start(sw2_sb[:], sw2).then_inc(shared_loaded, 16)
                if h == KR + 4:
                    sp.dma_start(w13_sb[:], w13).then_inc(experts_loaded, 16)
                    sp.dma_start(w2_sb[:], w2).then_inc(experts_loaded, 16)

            sp.wait_ge(pads_ready, 1)
            for e in range(E):
                first = sp.value_load(pad_row[0:1, e:e + 1], min_val=0, max_val=E * CAP - P)
                sp.dma_start(routed_in[bass.ds(first, P), :], empty[:, e]).then_inc(pads_stored, 16)

            sp.wait_ge(tile_rows_ready, 1)
            sp.wait_ge(rows_emptied, 16)
            sp.wait_ge(pads_stored, 16 * E)
            for s in range(ROUND):
                sp.wait_ge(scattered[s], 16 * TOPK * ((H - 1 - s) // ROUND + 1))
            for t in range(TILES):
                if t >= RR:
                    sp.wait_ge(rT_done, t - RR + 1)
                    sp.wait_ge(added[t % RO], 16 + 16 * ((t - RR) // RO + 1))
                first = sp.value_load(tile_row[0:1, t:t + 1], min_val=0, max_val=E * CAP + (E - 1) * P)
                sp.dma_start(r_in[:, t % RR], routed_in[bass.ds(first, P), :]).then_inc(r_loaded[t % RR], 16)

            for s in range(RO):
                sp.wait_ge(added[s], 16 + 16 * ((TILES - 1 - s) // RO + 1))

        @block.gpsimd
        def _(pool):
            nc.gpsimd.memset(ident[:], 0.0).then_inc(masks_set, 1)
            pool.wait_ge(masks_set, 1)
            nc.gpsimd.affine_select(out=ident[:], in_=ident[:], compare_op=ALU.not_equal, fill=1.0,
                                    base=0, pattern=[[-1, P]], channel_multiplier=1).then_inc(ident_ready, 1)

            def make_z(h):
                pool.wait_ge(keys_loaded[h % KR], 16 * (h // KR + 1))
                await_count(pool, y_done_b, (h - 1) * LB)
                for b in range(LB):
                    at = (h % KR * LB + b) * B * KW
                    last = nc.gpsimd.tensor_tensor(
                        z[:, h % 2, b, ROWS:PAIRS].rearrange("p (d b i) -> p d b i", d=D_FULL - 1, b=B),
                        view(keys, at, [(0, D_FULL - 1), (KW, B), (1, HD)]),
                        view(keys, at + 1, [(1, D_FULL - 1), (KW, B), (1, HD)]), ALU.mult)
                if opposite_on_pool(h):
                    at = h % KR * LB * B * KW
                    last = nc.gpsimd.tensor_tensor(
                        view(z, h % 2 * LB * ZW + PAIRS, [(ZW, LB), (HD // 2, B), (1, HD // 2)]),
                        view(keys, at, [(B * KW, LB), (KW, B), (1, HD // 2)]),
                        view(keys, at + HD // 2, [(B * KW, LB), (KW, B), (1, HD // 2)]), ALU.mult)
                last.then_inc(z_ready, 1)

            def send_rows(n):
                pool.wait_ge(slots_ready, group_of(n) + 1)
                pool.wait_ge(rows_ready, n + 1)
                pool.wait_ge(ids_ready, n + 1)
                for k in range(TOPK):
                    nc.gpsimd.indirect_dma_start(
                        routed_in, bass.IndirectOffsetOnAxis(ap=slot_of[:, k, n:n + 1].bitcast(U32), axis=0),
                        rows[:, n % ROUND, k], None).then_inc(scattered[n % ROUND], 16)

            make_z(0)
            make_z(1)
            nc.gpsimd.memset(before[:], 1.0).then_inc(masks_set, 1)
            pool.wait_ge(masks_set, 2)
            nc.gpsimd.affine_select(out=before[:], in_=before[:], compare_op=ALU.is_gt, fill=0.0,
                                    base=0, pattern=[[1, P]], channel_multiplier=-1)
            nc.gpsimd.memset(rows[:, :, :, L:RW], 0.0)
            nc.gpsimd.memset(ones[:], 1.0)
            nc.gpsimd.memset(ones_row[:], 1.0)
            nc.gpsimd.memset(mask[:], 0.0)
            nc.gpsimd.iota(next_row[:], [[CAP, E]], base=0, channel_multiplier=0,
                           allow_small_or_imprecise_dtypes=True)
            nc.gpsimd.iota(tile_at[:], [[P, TILES]], base=0, channel_multiplier=0,
                           allow_small_or_imprecise_dtypes=True)
            nc.gpsimd.iota(tile_adds[:], [[16, -(-TILES // RO)], [0, RO]], base=16, channel_multiplier=0,
                           allow_small_or_imprecise_dtypes=True)
            nc.gpsimd.iota(row_id[:], [[P, H], [0, 1]], base=0, channel_multiplier=1)
            nc.gpsimd.iota(down[:], [[-1, E]], base=E, channel_multiplier=0,
                           allow_small_or_imprecise_dtypes=True)
            nc.gpsimd.iota(fills[:], [[CAP, E], [P, H]], base=0, channel_multiplier=0,
                           allow_small_or_imprecise_dtypes=True)
            nc.gpsimd.iota(tile_id[:], [[1, TILES]], base=0, channel_multiplier=0,
                           allow_small_or_imprecise_dtypes=True).then_inc(consts_ready, 1)
            pool.wait_ge(empty_cleared, 1)
            nc.gpsimd.iota(empty[:, :, L:L + 1].bitcast(I32), [[P, SETS], [0, 1]], base=H * ROWS,
                           channel_multiplier=1).then_inc(empty_ready, 1)

            for h in range(H):
                pool.wait_ge(q_ready, h + 1)
                for b in range(LB):
                    pool.wait_ge(y_ready_b, h * LB + b + 1)
                    await_count(pool, att_ready_b, (h - 1) * LB + b + 1 if h else 0)
                    at_y = (h % 2 * LB + b) * (D_FULL + 1) * B * YW
                    at_q = (h % 2 * LB + b) * B * QW
                    nc.gpsimd.tensor_tensor(
                        view(prods, b * ROWS * HD + D_FULL + 1, [(1, D_FULL - 1), (HD * HD, B), (HD, HD)]),
                        view(y, at_y + B * YW + YPAD - 1, [(B * YW - 1, D_FULL - 1), (YW, B), (1, HD)]),
                        view(queries, at_q + YPAD - 1, [(-1, D_FULL - 1), (QW, B), (1, HD)]),
                        ALU.mult).then_inc(far_done_b, 1)
                for n in sent_at(h - 1):
                    send_rows(n)
                if h + 2 < H:
                    make_z(h + 2)
                if 4 < h <= 4 + RO:
                    s, n = h - 5, SETS // RO
                    pool.wait_ge(empty_ready, 1)
                    nc.gpsimd.dma_start(out[(H + s * n) * P:(H + (s + 1) * n) * P].rearrange("(n p) c -> p n c", p=P),
                                        empty[:, s * n:(s + 1) * n, 0:L]).then_inc(added[s], 16)

            for n in sent_at(H - 1) + sent_at(H) + sent_at(H + 1) + sent_at(H + 2) + list(range(EARLY, H)):
                send_rows(n)

            pool.wait_ge(bases_stored, 16 * NCHUNK)
            for s in range(RO):
                pool.wait_ge(added[s], 16)
            pool.wait_ge(adds_ready, 1)
            for t in range(TILES):
                if t:
                    in_round = pool.value_load(adds[0:1, 0, t:t + 1], min_val=16, max_val=16 * TILES)
                    if t >= RO:
                        in_last = pool.value_load(adds[0:1, 1, t:t + 1], min_val=16, max_val=16 * TILES)
                    for u in range(max(t - RO, 0), t):
                        pool.wait_ge(added[u % RO], in_round if u // RO == t // RO else in_last)
                    nc.gpsimd.tensor_tensor(waited[:, t:t + 1], ones_row[0:1, 0:1], ones_row[0:1, 0:1], ALU.mult)
                pool.wait_ge(ro_ready, t + 1)
                nc.gpsimd.indirect_dma_start(
                    out, bass.IndirectOffsetOnAxis(ap=r_in[:, t % RR, L:L + 1].bitcast(U32), axis=0),
                    r_out[:, t % RO], None, compute_op=ALU.add).then_inc(added[t % RO], 16)

        @block.scalar
        def _(act):
            act.dma_start(filt[:, P - 2:P - 1 + L], skip_and_taps).then_inc(taps_loaded, 16)
            act.dma_start(gates[:], both_gates.partition_broadcast(P)).then_inc(gates_loaded, 16)
            act.wait_ge(eps_ready, 1)
            nc.scalar.activation(spare_act[:, 0:1], eps[:], ACT.Tanh)
            act.wait_ge(gates_loaded, 16)
            nc.scalar.activation(tanh_g[:], gates[:], ACT.Tanh).then_inc(tanh_ready, 1)
            nc.scalar.activation(spare_act[:, 1:2], eps[:], ACT.Sqrt)

            def root_var1(c):
                act.wait_ge(var1_ready, NORM_END[c])
                now = slice(NORM_END[c] - NORMED[c], NORM_END[c])
                nc.scalar.activation(std1[:, now], mv1[:, now, 1], ACT.Sqrt, bias=eps[:, 0:1]).then_inc(std1_ready, 1)

            def make_squares(h):
                act.wait_ge(keys_loaded[h % KR], 16 * (h // KR + 1))
                await_count(act, y_done_b, (h - 1) * LB)
                nc.scalar.activation(
                    z[:, h % 2, :, 0:ROWS].rearrange("p m (b i) -> p m b i", b=B),
                    view(keys, h % KR * LB * B * KW, [(B * KW, LB), (KW, B), (1, HD)]), ACT.Square)\
                    .then_inc(squares_ready, 1)

            def norm_x(h):
                act.wait_ge(shift1_ready, sum(1 for end in NORM_END if end <= h) + 1)
                await_count(act, q_done, h - 1)
                nc.scalar.activation(xq[:, h % 2], x_all[:, h], ACT.Identity, bias=shift1[:, h:h + 1],
                                     scale=rstd1[:, h:h + 1]).then_inc(xq_ready, 1)

            def load_queries(h):
                act.wait_ge(q_done, h + 1)
                await_count(act, near_done_b, (h - 1) * LB)
                await_count(act, far_done_b, (h - 1) * LB)
                src = q_ps.rearrange("p (r i) -> p r i", i=HD)
                dst = queries[:, h % 2].rearrange("p l (b i) -> p (l b) i", i=QW)
                nc.scalar.activation(dst[:, :, YPAD:YPAD + HD], src, ACT.Copy)
                nc.scalar.activation(dst[:, :, 0:YPAD], src[:, :, HD - YPAD:HD], ACT.Copy)
                nc.scalar.activation(dst[:, :, YPAD + HD:YPAD + HD + D_FULL], src[:, :, 0:D_FULL], ACT.Copy)\
                    .then_inc(q_ready, 1)

            def load_y(h, b):
                act.wait_ge(y_done_b, h * LB + b + 1)
                if h >= 2:
                    act.wait_ge(near_done_b, (h - 2) * LB + b + 1)
                    act.wait_ge(far_done_b, (h - 2) * LB + b + 1)
                src = y_ps[b][:, :].rearrange("p (r i) -> p r i", i=HD)
                dst = y[:, h % 2, b].rearrange("p (r i) -> p r i", i=YW)
                nc.scalar.activation(dst[:, 0:D_FULL * B, YPAD:YW], src, ACT.Copy)
                nc.scalar.activation(dst[:, B:D_FULL * B, 0:YPAD], src[:, B:D_FULL * B, HD - YPAD:HD], ACT.Copy)
                src4 = y4_ps[b]
                nc.scalar.activation(
                    view(y, ((h % 2 * LB + b) * (D_FULL + 1) + D_FULL) * B * YW + YPAD,
                         [(YW, B), (HD // 2, 2), (1, HD // 2)]),
                    bass.AP(src4.tensor, src4.offset, [list(src4.ap[0]), [HD // 2, B], [0, 2], [1, HD // 2]]),
                    ACT.Copy).then_inc(y_ready_b, 1)

            def deviation(h):
                act.wait_ge(mv_ready, h + 1)
                await_count(act, rstd_ready, h - 1)
                nc.scalar.activation(std2[:, h % 2:h % 2 + 1], mv2[:, h % 2, 1:2], ACT.Sqrt,
                                     bias=eps[:, 0:1]).then_inc(std_ready, 1)

            def norm_x1(h):
                act.wait_ge(shift_ready, h + 1)
                nc.scalar.activation(xn_all[:, h], x_all[:, h], ACT.Identity, bias=shift2[:, h % 2:h % 2 + 1],
                                     scale=rstd2[:, h % 2:h % 2 + 1]).then_inc(xn_ready, 1)

            def load_xnT(h):
                act.wait_ge(xnT_done, h + 1)
                nc.scalar.activation(xnT_all[:, :, h * P:(h + 1) * P], xnT_ps.rearrange("p (c t) -> p c t", c=LB),
                                     ACT.Copy).then_inc(xnT_ready, 1)

            def load_logits(h):
                act.wait_ge(gate_done, h + 1)
                nc.scalar.activation(logits[:, h], gate_ps, ACT.Copy).then_inc(logits_ready, 1)

            def squash(g):
                heads = slice(GROUP_END[g] - GROUPS[g], GROUP_END[g])
                act.wait_ge(logits_ready, GROUP_END[g])
                nc.scalar.activation(probs[:, heads], logits[:, heads], ACT.Sigmoid).then_inc(probs_ready, 1)

            def load_place(g):
                act.wait_ge(place_done, g + 1)
                nc.scalar.activation(place[:, g, 0:GROUPS[g] + 1], place_ps[:, 0:(GROUPS[g] + 1) * E]
                                     .rearrange("p (h e) -> p h e", e=E), ACT.Copy).then_inc(place_ready, 1)

            def make_rows(n):
                if n == GROUP_END[group_of(n)] - GROUPS[group_of(n)]:
                    act.wait_ge(mask_ready, group_of(n) + 1)
                await_count(act, scattered[n % ROUND], 16 * TOPK * (n // ROUND))
                for k in range(TOPK):
                    last = nc.scalar.activation(rows[:, n % ROUND, k, 0:L], xn_all[:, n], ACT.Copy,
                                                scale=score[:, n, k:k + 1])
                last.then_inc(rows_ready, 1)

            make_squares(0)
            root_var1(0)
            norm_x(0)
            make_squares(1)
            norm_x(1)
            load_queries(0)
            for h in range(H + 3):
                if h < H:
                    load_y(h, 0)
                if 2 <= h < H + 2:
                    norm_x1(h - 2)
                if h == H + 1:
                    nc.scalar.activation(spare_act[:, 2:3], eps[:], ACT.Sigmoid)
                if h < H:
                    load_y(h, 1)
                if h + 2 < H:
                    make_squares(h + 2)
                if h + 1 < H:
                    load_queries(h + 1)
                if h - SEND_LAG + 1 in GROUP_END[:-1]:
                    load_place(group_of(h - SEND_LAG))
                for n in sent_at(h) if h <= H else []:
                    make_rows(n)
                for c in starting(3, h):
                    root_var1(c)
                if 1 <= h < H + 1:
                    deviation(h - 1)
                if h >= 3:
                    load_logits(h - 3)
                    if h == H + 2:
                        squash(len(GROUPS) - 1)
                if 2 <= h < H + 2:
                    load_xnT(h - 2)
                if h + 2 < H:
                    norm_x(h + 2)
                for n in sent_at(h) if h > H else []:
                    make_rows(n)
                if h - 2 in GROUP_END[:-1]:
                    squash(group_of(h - 3))

            def store_bases(c):
                act.wait_ge(base_ready, CHUNK * (c + 1))
                act.dma_start(out[c * CHUNK * P:(c + 1) * CHUNK * P].rearrange("(h p) c -> p h c", p=P),
                              xn_all[:, c * CHUNK:(c + 1) * CHUNK]).then_inc(bases_stored, 16)

            for c in range(NCHUNK):
                if c == 3:
                    store_bases(0)
                if c == 2:
                    make_rows(EARLY)
                    make_rows(EARLY + 1)
                    load_place(len(GROUPS) - 1)
                    for n in range(EARLY + 2, min(EARLY + ROUND, H)):
                        make_rows(n)
                if c >= 2:
                    for n in late_rows(c):
                        make_rows(n)
                act.wait_ge(up_done, 2 * c + 1)
                await_count(act, sh_ready, c - 1)
                nc.scalar.activation(shared_act[:, c % 2], up_ps[c % 2][0][:, :], ACT.Silu)\
                    .then_inc(sact_ready, 1)

            for t in range(TILES + 3):
                if t < TILES:
                    act.wait_ge(rT_done, t + 1)
                    await_count(act, ru_done, t - 1)
                    nc.scalar.activation(r_inT[:, t % 2], rT_ps[t % 2].rearrange("p (c t) -> p c t", c=LB),
                                         ACT.Copy).then_inc(rT_ready, 1)
                if 1 <= t < NCHUNK:
                    store_bases(t)
                u = t - 1
                if 0 <= u < TILES:
                    act.wait_ge(ru_done, u + 1)
                    await_count(act, rh_ready, u - 1)
                    nc.scalar.activation(r_act[:, u % 2], ru_ps[u % 2][:, 0:HID], ACT.Silu).then_inc(ract_ready, 1)
                v = t - 3
                if v >= 0:
                    act.wait_ge(ro_done, v + 1)
                    if v >= RO:
                        act.wait_ge(added[v % RO], 16 + 16 * (v // RO))
                    nc.scalar.activation(r_out[:, v % RO], ro_ps[v % 2], ACT.Copy, scale=tanh_g[:, 1:2])\
                        .then_inc(ro_ready, 1)

        @block.vector
        def _(dve):
            nc.vector.memset(filt[:, 0:P - 2], 0.0)
            nc.vector.memset(filt[:, P - 1 + L:KPAD], 0.0).then_inc(filt_zeroed, 1)
            nc.vector.memset(eps[:], EPS).then_inc(eps_ready, 1)
            dve.wait_ge(taps_loaded, 16)
            dve.wait_ge(filt_zeroed, 1)
            nc.vector.tensor_tensor(filt[:, P - 1:P], filt[:, P - 1:P], filt[:, P - 2:P - 1], ALU.add)\
                .then_inc(skip_added, 1)
            dve.wait_ge(skip_added, 1)
            nc.vector.memset(filt[:, P - 2:P - 1], 0.0).then_inc(filt_ready, 1)

            def variances(heads):
                for h in heads:
                    if h in [0] + NORM_END:
                        dve.wait_ge(x_loaded[([0] + NORM_END).index(h)], 16)
                    nc.vector.bn_stats(st1[:, h], x_all[:, h]).then_inc(stats1_ready, 1)
                for h in heads:
                    dve.wait_ge(stats1_ready, h + 1)
                    nc.vector.bn_aggr(mv1[:, h], st1[:, h]).then_inc(var1_ready, 1)

            def shifts(c):
                now = slice(NORM_END[c] - NORMED[c], NORM_END[c])
                dve.wait_ge(std1_ready, c + 1)
                nc.vector.reciprocal(rstd1[:, now], std1[:, now]).then_inc(rstd1_ready, 1)
                dve.wait_ge(rstd1_ready, c + 1)
                nc.vector.scalar_tensor_tensor(shift1[:, now], mv1[:, now, 0], -1.0, rstd1[:, now],
                                               ALU.mult, ALU.mult).then_inc(shift1_ready, 1)

            def make_opposite(h):
                dve.wait_ge(keys_loaded[h % KR], 16 * (h // KR + 1))
                await_count(dve, y_done_b, (h - 1) * LB)
                at = h % KR * LB * B * KW
                nc.vector.tensor_tensor(
                    view(z, h % 2 * LB * ZW + PAIRS, [(ZW, LB), (HD // 2, B), (1, HD // 2)]),
                    view(keys, at, [(B * KW, LB), (KW, B), (1, HD // 2)]),
                    view(keys, at + HD // 2, [(B * KW, LB), (KW, B), (1, HD // 2)]), ALU.mult)\
                    .then_inc(opposite_ready, 1)

            def near(h, b):
                dve.wait_ge(y_ready_b, h * LB + b + 1)
                if h:
                    dve.wait_ge(att_ready_b, (h - 1) * LB + b + 1)
                at_y = (h % 2 * LB + b) * (D_FULL + 1) * B * YW
                at_q = (h % 2 * LB + b) * B * QW
                nc.vector.tensor_tensor(
                    view(prods, b * ROWS * HD, [(1, D_FULL + 1), (HD * HD, B), (HD, HD)]),
                    view(y, at_y + YPAD, [(B * YW, D_FULL + 1), (YW, B), (1, HD)]),
                    view(queries, at_q + YPAD, [(1, D_FULL + 1), (QW, B), (1, HD)]),
                    ALU.mult).then_inc(near_done_b, 1)

            def attend(h, b):
                dve.wait_ge(near_done_b, h * LB + b + 1)
                dve.wait_ge(far_done_b, h * LB + b + 1)
                await_count(dve, att_done, h - 1)
                if PARTS[b] == 1:
                    nc.vector.tensor_reduce(att[:, h % 2, b, 0], prods[:, b].rearrange("p (r t) -> p r t", t=HD),
                                            AX_X, ALU.add).then_inc(att_ready_b, 1)
                else:
                    pairs = prods[:, b].rearrange("p (r t) -> p t r", t=HD)
                    nc.vector.tensor_tensor(att[:, h % 2, b], pairs[:, 0:HD // 2], pairs[:, HD // 2:HD], ALU.add)\
                        .then_inc(att_ready_b, 1)

            def add_attention(h):
                dve.wait_ge(att_done, h + 1)
                nc.vector.scalar_tensor_tensor(x_all[:, h], att_ps, tanh_g[:, 0:1], x_all[:, h], ALU.mult, ALU.add)\
                    .then_inc(x1_ready, 1)
                dve.wait_ge(x1_ready, h + 1)
                nc.vector.bn_stats(st2[:, h % 2], x_all[:, h]).then_inc(stats_ready, 1)
                dve.wait_ge(stats_ready, h + 1)
                await_count(dve, std_ready, h - 1)
                await_count(dve, shift_ready, h - 1)
                nc.vector.bn_aggr(mv2[:, h % 2], st2[:, h % 2]).then_inc(mv_ready, 1)

            def shift_x1(h):
                dve.wait_ge(std_ready, h + 1)
                await_count(dve, xn_ready, h - 1)
                nc.vector.reciprocal(rstd2[:, h % 2:h % 2 + 1], std2[:, h % 2:h % 2 + 1]).then_inc(rstd_ready, 1)
                dve.wait_ge(rstd_ready, h + 1)
                nc.vector.scalar_tensor_tensor(shift2[:, h % 2:h % 2 + 1], mv2[:, h % 2, 0:1], -1.0,
                                               rstd2[:, h % 2:h % 2 + 1], ALU.mult, ALU.mult)\
                    .then_inc(shift_ready, 1)

            steps = [0]

            def link(ins):
                steps[0] += 1
                ins.then_inc(route, 1)
                dve.wait_ge(route, steps[0])

            def choose(g, k):
                heads, n = slice(GROUP_END[g] - GROUPS[g], GROUP_END[g]), GROUPS[g]
                of = (probs, rest)[k]
                if g == 0:
                    dve.wait_ge(consts_ready, 1)
                dve.wait_ge(probs_ready, g + 1)
                down_b = view(down, 0, [(0, n), (1, E)])
                link(nc.vector.tensor_reduce(score[:, heads, k], of[:, heads], AX_X, ALU.max))
                link(nc.vector.tensor_tensor(is_max[:, heads], of[:, heads],
                                             score[:, heads, k:k + 1].broadcast_to([P, n, E]), ALU.is_equal))
                link(nc.vector.tensor_tensor(rank[:, heads], is_max[:, heads], down_b, ALU.mult))
                link(nc.vector.tensor_reduce(top_rank[:, heads, k], rank[:, heads], AX_X, ALU.max))
                link(nc.vector.tensor_tensor(chosen[:, k, heads], down_b,
                                             top_rank[:, heads, k:k + 1].broadcast_to([P, n, E]), ALU.is_equal))
                if k == 0:
                    link(nc.vector.scalar_tensor_tensor(rest[:, heads], chosen[:, 0, heads], -2.0,
                                                        probs[:, heads], ALU.mult, ALU.add))
                else:
                    nc.vector.tensor_tensor(mask[:, g, 0:n * E].rearrange("p (h e) -> p h e", e=E),
                                            chosen[:, 0, heads], chosen[:, 1, heads], ALU.add)\
                        .then_inc(mask_ready, 1)

            def find_slots(g):
                heads, n = slice(GROUP_END[g] - GROUPS[g], GROUP_END[g]), GROUPS[g]
                dve.wait_ge(place_ready, g + 1)
                link(nc.vector.tensor_tensor(at_row[:, 0:n], place[:, g, 0:n], view(next_row, 0, [(0, n), (1, E)]),
                                             ALU.add))
                nc.vector.tensor_tensor(next_row[:], next_row[:], place[:, g, n], ALU.add)
                link(nc.vector.tensor_tensor(picked[:, :, 0:n], chosen[:, :, heads],
                                             view(at_row, 0, [(0, TOPK), (E, n), (1, E)]), ALU.mult))
                link(nc.vector.tensor_reduce(slot_f[:, :, heads], picked[:, :, 0:n], AX_X, ALU.add))
                nc.vector.tensor_copy(slot_of[:, :, heads], slot_f[:, :, heads]).then_inc(slots_ready, 1)

            def mark_rows(n):
                await_count(dve, scattered[n % ROUND], 16 * TOPK * (n // ROUND))
                nc.vector.tensor_copy(rows[:, n % ROUND, :, L:L + 1].bitcast(I32),
                                      row_id[:, n:n + 1].broadcast_to([P, TOPK, 1]))\
                    .then_inc(ids_ready, 1)

            variances(range(NORMED[0]))
            shifts(0)
            nc.vector.memset(empty[:], 0.0).then_inc(empty_cleared, 1)
            dve.wait_ge(tanh_ready, 1)
            for h in range(H + 1):
                if h < H:
                    dve.wait_ge(q_ready, h + 1)
                    near(h, 0)
                variances([n for n in range(NORMED[0], H) if measured_at(n) == h])
                if h - 3 in GROUP_END[:-1]:
                    choose(group_of(h - 4), 0)
                if h < H:
                    attend(h, 0)
                if h >= 1:
                    add_attention(h - 1)
                if h < H:
                    near(h, 1)
                if h + 2 < H and not opposite_on_pool(h + 2):
                    make_opposite(h + 2)
                for c in starting(3, h):
                    shifts(c)
                if h >= 1:
                    shift_x1(h - 1)
                if h - 3 in GROUP_END[:-1]:
                    choose(group_of(h - 4), 1)
                if h - SEND_LAG + 1 in GROUP_END[:-1]:
                    find_slots(group_of(h - SEND_LAG))
                for n in sent_at(h) + (sent_at(H + 1) + sent_at(H + 2) if h == H else []):
                    mark_rows(n)
                if h < H:
                    attend(h, 1)

            def gate_shared(c):
                dve.wait_ge(sact_ready, c + 1)
                await_count(dve, sout_done, CHUNK * (c - 1))
                dve.wait_ge(up_done, 2 * (c + 1))
                nc.vector.tensor_tensor(shared_h[:, c % 2], shared_act[:, c % 2], up_ps[c % 2][1][:, :], ALU.mult)\
                    .then_inc(sh_ready, 1)

            last_group = len(GROUPS) - 1
            choose(last_group, 0)
            choose(last_group, 1)
            gate_shared(0)
            for n in range(EARLY, EARLY + 2):
                mark_rows(n)
            find_slots(last_group)
            for n in range(EARLY + 2, min(EARLY + ROUND, H)):
                mark_rows(n)
            nc.vector.tensor_copy(pad_row[:], next_row[0:1]).then_inc(pads_ready, 1)

            def find_tiles():
                link(nc.vector.tensor_tensor(over[:], on_first(next_row, [(1, E), (0, H)]),
                                             on_first(fills, [(H, E), (1, H)]), ALU.is_gt))
                link(nc.vector.tensor_reduce(tiles[:], over[:], AX_X, ALU.add))
                link(nc.vector.tensor_tensor_scan(tiles_to[:], ones_row[0:1], tiles[:], 0.0, ALU.mult, ALU.add))
                nc.vector.tensor_scalar(skipped[:], tiles[:], -float(P), float(CAP), ALU.mult, ALU.add)
                link(nc.vector.tensor_tensor(ended[:], on_first(tiles_to, [(0, TILES), (1, E)]),
                                             on_first(tile_id, [(1, TILES), (0, E)]), ALU.is_le))
                link(nc.vector.tensor_reduce(tile_expert_f[:], ended[:], AX_X, ALU.add))
                nc.vector.tensor_scalar(tile_expert[:], tile_expert_f[:], float(E - 1), None, ALU.min)\
                    .then_inc(table_ready, 1)
                link(nc.vector.tensor_tensor(jumps[:], ended[:], on_first(skipped, [(0, TILES), (1, E)]), ALU.mult))
                link(nc.vector.tensor_reduce(jump[:], jumps[:], AX_X, ALU.add))
                link(nc.vector.tensor_tensor(tile_row_f[:], jump[:], tile_at[0:1], ALU.add))
                nc.vector.tensor_copy(tile_row[:], tile_row_f[:]).then_inc(tile_rows_ready, 1)
                nc.vector.memset(new_expert[:, 0:1], 0.0)
                link(nc.vector.tensor_tensor(new_expert[:, 1:TILES], tile_expert_f[:, 1:TILES],
                                             tile_expert_f[:, 0:TILES - 1], ALU.not_equal))
                link(nc.vector.scalar_tensor_tensor(adds_f[:], new_expert[:], 16.0, on_first(tile_adds, [(1, TILES)]),
                                                    ALU.mult, ALU.add))
                nc.vector.tensor_copy(adds[:, 0], adds_f[:])
                nc.vector.tensor_scalar(adds[:, 1], adds_f[:], -16.0, None, ALU.add).then_inc(adds_ready, 1)

            gate_shared(1)
            for c in range(NCHUNK):
                if c >= 2:
                    gate_shared(c)
                for n in range(CHUNK * c, CHUNK * c + CHUNK):
                    dve.wait_ge(sout_done, n + 1)
                    dve.wait_ge(rows_ready, n + 1)
                    nc.vector.scalar_tensor_tensor(xn_all[:, n], sh_ps[n % CHUNK], tanh_g[:, 1:2], x_all[:, n],
                                                   ALU.mult, ALU.add).then_inc(base_ready, 1)
                if c == 0:
                    find_tiles()
                if c + 1 in (2, 3):
                    for n in late_rows(c + 1):
                        mark_rows(n)

            for t in range(TILES + 2):
                w = t - 2
                if w >= 0:
                    dve.wait_ge(rhT_done, w + 1)
                    await_count(dve, ro_done, w - 1)
                    nc.vector.tensor_copy(r_hT[:, w % 2], rh_ps[w % 2]).then_inc(rhT_ready, 1)
                u = t - 1
                if 0 <= u < TILES:
                    dve.wait_ge(ract_ready, u + 1)
                    await_count(dve, rhT_done, u - 1)
                    nc.vector.tensor_tensor(r_h[:, u % 2], r_act[:, u % 2], ru_ps[u % 2][:, HID:2 * HID],
                                            ALU.mult).then_inc(rh_ready, 1)

        @block.tensor
        def _(pe):
            def transpose_q(h):
                pe.wait_ge(xq_ready, h + 1)
                await_count(pe, q_ready, h)
                for b in range(LB):
                    last = nc.tensor.transpose(q_ps[:, b * P:(b + 1) * P], xq[:, h % 2, b * P:(b + 1) * P], ident[:])
                last.then_inc(q_done, 1)

            def convolve(h):
                pe.wait_ge(toep_loaded[h % KR], 16 * (h // KR + 1))
                pe.wait_ge(z_ready, h + 1)
                pe.wait_ge(squares_ready, h + 1)
                await_count(pe, opposite_ready, sum(not opposite_on_pool(n) for n in range(h + 1)))
                same, previous = toep[:, h % KR, 0:P], toep[:, h % KR, P:2 * P]
                for b, terms in enumerate([[(same, 0)], [(previous, 0), (same, 1)]]):
                    if h:
                        pe.wait_ge(y_ready_b, (h - 1) * LB + b + 1)
                    for n, (w, m) in enumerate(terms):
                        flags = dict(start=(n == 0), stop=(n == len(terms) - 1))
                        nc.tensor.matmul(y_ps[b][:, :], w, z[:, h % 2, m, 0:PAIRS], **flags)
                        last = nc.tensor.matmul(y4_ps[b], w, z[:, h % 2, m, PAIRS:ZW], **flags)
                    last.then_inc(y_done_b, 1)

            def transpose_att(h):
                pe.wait_ge(att_ready_b, (h + 1) * LB)
                await_count(pe, x1_ready, h)
                for b in range(LB):
                    for n in range(PARTS[b]):
                        last = nc.tensor.matmul(att_ps[:, b * P:(b + 1) * P], att[:, h % 2, b, n], ident[:],
                                                start=(n == 0), stop=(n == PARTS[b] - 1))
                last.then_inc(att_done, 1)

            def transpose_xn(h):
                pe.wait_ge(xn_ready, h + 1)
                await_count(pe, xnT_ready, h)
                for b in range(LB):
                    last = nc.tensor.transpose(xnT_ps[:, b * P:(b + 1) * P], xn_all[:, h, b * P:(b + 1) * P], ident[:])
                last.then_inc(xnT_done, 1)

            def gate(h):
                pe.wait_ge(xnT_ready, h + 1)
                await_count(pe, logits_ready, h)
                await_count(pe, place_ready, sum(1 for end in GROUP_END[:-1] if end + SEND_LAG - 1 <= h + 3))
                for b in range(LB):
                    last = nc.tensor.matmul(gate_ps, xnT_all[:, b, h * P:(h + 1) * P], gate_sb[:, b], start=(b == 0),
                                            stop=(b == LB - 1))
                last.then_inc(gate_done, 1)

            def count_rows(g):
                n = GROUPS[g]
                if g == 0:
                    pe.wait_ge(consts_ready, 1)
                pe.wait_ge(mask_ready, g + 1)
                nc.tensor.matmul(place_ps[:, 0:(n + 1) * E], before[:], mask[:, g, 0:(n + 1) * E], start=True,
                                 stop=False)
                for h in range(n):
                    last = nc.tensor.matmul(place_ps[:, (h + 1) * E:(n + 1) * E], ones[:],
                                            view(mask, (g * (GROUP_MAX + 1) + h) * E, [(0, n - h), (1, E)]),
                                            start=False, stop=(h == n - 1))
                last.then_inc(place_done, 1)

            def up(c, j):
                await_count(pe, sh_ready, c - 1)
                for b in range(LB):
                    last = nc.tensor.matmul(up_ps[c % 2][j][:, :], sw13_sb[:, b, j * HID:(j + 1) * HID],
                                            xnT_all[:, b, c * CHUNK * P:(c + 1) * CHUNK * P],
                                            start=(b == 0), stop=(b == LB - 1))
                last.then_inc(up_done, 1)

            pe.wait_ge(ident_ready, 1)
            transpose_q(0)
            for h in range(H + 3):
                if h < H:
                    convolve(h)
                if h == H:
                    pe.wait_ge(shared_loaded, 32)
                    pe.wait_ge(y_ready_b, H * LB)
                    up(0, 0)
                    up(0, 1)
                if h == H + 1:
                    up(1, 0)
                if h == H + 2:
                    up(1, 1)
                if h + 1 < H:
                    transpose_q(h + 1)
                if 1 <= h < H + 1:
                    transpose_att(h - 1)
                if h - SEND_LAG + 1 in GROUP_END[:-1]:
                    pe.wait_ge(logits_ready, h - 3)
                    count_rows(group_of(h - SEND_LAG))
                if h == 3:
                    pe.wait_ge(gatew_loaded, 16)
                if h >= 3:
                    gate(h - 3)
                if 2 <= h < H + 2:
                    transpose_xn(h - 2)

            pe.wait_ge(logits_ready, H)
            count_rows(len(GROUPS) - 1)
            pe.wait_ge(place_ready, len(GROUPS))
            pe.wait_ge(x1_ready, H)
            for c in range(NCHUNK):
                pe.wait_ge(sh_ready, c + 1)
                for t in range(CHUNK):
                    await_count(pe, base_ready, CHUNK * (c - 1) + t + 1)
                    nc.tensor.matmul(sh_ps[t], shared_h[:, c % 2, t * P:(t + 1) * P], sw2_sb[:], start=True,
                                     stop=True).then_inc(sout_done, 1)
                if c + 2 < NCHUNK:
                    up(c + 2, 0)
                    up(c + 2, 1)

            pe.wait_ge(experts_loaded, 32)
            pe.wait_ge(table_ready, 1)
            pe.wait_ge(base_ready, H)
            pe.wait_ge(sh_ready, NCHUNK)
            expert = {}
            for t in range(TILES + 3):
                if t < TILES:
                    expert[t] = pe.value_load(tile_expert[0:1, t:t + 1], min_val=0, max_val=E - 1)
                    pe.wait_ge(r_loaded[t % RR], 16 * (t // RR + 1))
                    await_count(pe, rT_ready, t - 1)
                    for b in range(LB):
                        last = nc.tensor.transpose(rT_ps[t % 2][:, b * P:(b + 1) * P],
                                                   r_in[:, t % RR, b * P:(b + 1) * P], ident[:])
                    last.then_inc(rT_done, 1)
                u = t - 1
                if 0 <= u < TILES:
                    pe.wait_ge(rT_ready, u + 1)
                    await_count(pe, rh_ready, u - 1)
                    for b in range(LB):
                        last = nc.tensor.matmul(ru_ps[u % 2], r_inT[:, u % 2, b],
                                                w13_sb[:, b, bass.ds(expert[u] * (2 * HID), 2 * HID)],
                                                start=(b == 0), stop=(b == LB - 1))
                    last.then_inc(ru_done, 1)
                v = t - 3
                if v >= 0:
                    pe.wait_ge(rhT_ready, v + 1)
                    await_count(pe, ro_ready, v - 1)
                    nc.tensor.matmul(ro_ps[v % 2], r_hT[:, v % 2], w2_sb[:, bass.ds(expert.pop(v) * L, L)],
                                     start=True, stop=True).then_inc(ro_done, 1)
                w = t - 2
                if 0 <= w < TILES:
                    pe.wait_ge(rh_ready, w + 1)
                    await_count(pe, rhT_ready, w - 1)
                    nc.tensor.transpose(rh_ps[w % 2], r_h[:, w % 2], ident[:]).then_inc(rhT_done, 1)


def kernel(x, ctx_2048, g_xattn, g_ffn, L0_xattn_ssm_kernel, L0_xattn_D, L0_ffn_gate_w, L0_ffn_w1, L0_ffn_w2,
           L0_ffn_w3, L0_ffn_sw1, L0_ffn_sw2, L0_ffn_sw3):
    import numpy as np
    import concourse.bacc as bacc
    from concourse.bass_utils import run_bass_kernel_spmd

    def kmajor(w):
        return w.T.reshape(LB, P, -1).transpose(1, 0, 2)

    xs = x.reshape(B, H, HD, L).transpose(0, 2, 1, 3).reshape(P, H, L)
    c = ctx_2048.reshape(B, H, HD, LB, P)[..., ::-1].transpose(1, 4, 3, 0, 2)
    c = np.concatenate([c, c[..., :D_FULL]], axis=-1).reshape(H, P, LB, B * KW)
    w13 = np.stack([np.concatenate([kmajor(L0_ffn_w1[e]), kmajor(L0_ffn_w3[e])], axis=-1) for e in range(E)], axis=2)
    arrays = {
        "x": xs,
        "ctx": c,
        "both_gates": np.concatenate([g_xattn, g_ffn]),
        "skip_and_taps": np.concatenate([L0_xattn_D.reshape(H, 1), L0_xattn_ssm_kernel], axis=1),
        "gate_w": kmajor(L0_ffn_gate_w),
        "w13": w13.reshape(P, LB, E * 2 * HID),
        "w2": L0_ffn_w2.transpose(2, 0, 1).reshape(HID, E * L),
        "sw13": np.concatenate([kmajor(L0_ffn_sw1), kmajor(L0_ffn_sw3)], axis=-1),
        "sw2": L0_ffn_sw2.T,
    }
    arrays = {name: np.ascontiguousarray(a) for name, a in arrays.items()}
    nc = bacc.Bacc("TRN2", target_bir_lowering=False, num_devices=1)
    aps = [nc.dram_tensor(f"in_{name}", a.shape, mybir.dt.from_np(a.dtype), kind="ExternalInput").ap()
           for name, a in arrays.items()]
    out = nc.dram_tensor("out", [H * P + SETS * P, L], F32, kind="ExternalOutput").ap()
    flamingo_block(nc, *aps, out)
    done = run_bass_kernel_spmd(nc, [{f"in_{name}": a for name, a in arrays.items()}], core_ids=[0])
    got = done.results[0]["out"]
    got = got[:H * P].reshape(H, B, HD, L)
    return np.ascontiguousarray(got.transpose(1, 0, 2, 3).reshape(B, H * HD, L))
```
